# Optimizing a Trainium2 kernel written in Bass

```python
import numpy as np
import jax
import jax.numpy as jnp

def _softmax(x, axis=-1):
    return jax.nn.softmax(x, axis=axis)

def _gelu(x):
    return jax.nn.gelu(x, approximate=True)

def _silu(x):
    return jax.nn.silu(x)

def _sigmoid(x):
    return jax.nn.sigmoid(x)

def _layernorm(x, axis=-1, eps=1e-05):
    m = jnp.mean(x, axis=axis, keepdims=True)
    v = jnp.var(x, axis=axis, keepdims=True)
    return (x - m) / jnp.sqrt(v + eps)

def _scatter_add(tgt, idx, src, axis=0):
    return tgt.at[idx].add(src)

def _segment_sum(src, seg, n):
    return jax.ops.segment_sum(src, seg, n)
kernel_name = 'mk_dlrm_tower_d1_rec_r8_2860ea'

def setup_inputs(seed: int=0):
    np.random.seed(seed)
    _w = jnp.asarray

    def _rec_inputs():
        import jax
        import jax.numpy as jnp
        _tk = jax.random.key(seed)
        dense_ctx = jax.random.normal(jax.random.fold_in(_tk, 190), (1024, 16), jnp.float32)
        ids = jnp.stack([jax.random.randint(jax.random.fold_in(_tk, 200 + f), (1024,), 0, v, jnp.int32) for f, v in enumerate([1000, 125000, 1000, 1000, 1000, 12500, 1250, 1000, 1000, 1000, 1250, 1000, 1000, 1000, 12500, 1000, 125000, 12500, 1250, 1000, 1250, 1250, 12500, 12500, 12500, 12500, 12500, 125000, 1000, 1000, 1250, 12500, 1250, 1000, 12500, 1000, 1000, 12500, 125000])], axis=1)
        tbl_0 = 0.05 * jax.random.normal(jax.random.fold_in(_tk, 500 + 0), (1000, 16), jnp.float32)
        tbl_1 = 0.05 * jax.random.normal(jax.random.fold_in(_tk, 500 + 1), (125000, 16), jnp.float32)
        tbl_2 = 0.05 * jax.random.normal(jax.random.fold_in(_tk, 500 + 2), (1000, 16), jnp.float32)
        tbl_3 = 0.05 * jax.random.normal(jax.random.fold_in(_tk, 500 + 3), (1000, 16), jnp.float32)
        tbl_4 = 0.05 * jax.random.normal(jax.random.fold_in(_tk, 500 + 4), (1000, 16), jnp.float32)
        tbl_5 = 0.05 * jax.random.normal(jax.random.fold_in(_tk, 500 + 5), (12500, 16), jnp.float32)
        tbl_6 = 0.05 * jax.random.normal(jax.random.fold_in(_tk, 500 + 6), (1250, 16), jnp.float32)
        tbl_7 = 0.05 * jax.random.normal(jax.random.fold_in(_tk, 500 + 7), (1000, 16), jnp.float32)
        tbl_8 = 0.05 * jax.random.normal(jax.random.fold_in(_tk, 500 + 8), (1000, 16), jnp.float32)
        tbl_9 = 0.05 * jax.random.normal(jax.random.fold_in(_tk, 500 + 9), (1000, 16), jnp.float32)
        tbl_10 = 0.05 * jax.random.normal(jax.random.fold_in(_tk, 500 + 10), (1250, 16), jnp.float32)
        tbl_11 = 0.05 * jax.random.normal(jax.random.fold_in(_tk, 500 + 11), (1000, 16), jnp.float32)
        tbl_12 = 0.05 * jax.random.normal(jax.random.fold_in(_tk, 500 + 12), (1000, 16), jnp.float32)
        tbl_13 = 0.05 * jax.random.normal(jax.random.fold_in(_tk, 500 + 13), (1000, 16), jnp.float32)
        tbl_14 = 0.05 * jax.random.normal(jax.random.fold_in(_tk, 500 + 14), (12500, 16), jnp.float32)
        tbl_15 = 0.05 * jax.random.normal(jax.random.fold_in(_tk, 500 + 15), (1000, 16), jnp.float32)
        tbl_16 = 0.05 * jax.random.normal(jax.random.fold_in(_tk, 500 + 16), (125000, 16), jnp.float32)
        tbl_17 = 0.05 * jax.random.normal(jax.random.fold_in(_tk, 500 + 17), (12500, 16), jnp.float32)
        tbl_18 = 0.05 * jax.random.normal(jax.random.fold_in(_tk, 500 + 18), (1250, 16), jnp.float32)
        tbl_19 = 0.05 * jax.random.normal(jax.random.fold_in(_tk, 500 + 19), (1000, 16), jnp.float32)
        tbl_20 = 0.05 * jax.random.normal(jax.random.fold_in(_tk, 500 + 20), (1250, 16), jnp.float32)
        tbl_21 = 0.05 * jax.random.normal(jax.random.fold_in(_tk, 500 + 21), (1250, 16), jnp.float32)
        tbl_22 = 0.05 * jax.random.normal(jax.random.fold_in(_tk, 500 + 22), (12500, 16), jnp.float32)
        tbl_23 = 0.05 * jax.random.normal(jax.random.fold_in(_tk, 500 + 23), (12500, 16), jnp.float32)
        tbl_24 = 0.05 * jax.random.normal(jax.random.fold_in(_tk, 500 + 24), (12500, 16), jnp.float32)
        tbl_25 = 0.05 * jax.random.normal(jax.random.fold_in(_tk, 500 + 25), (12500, 16), jnp.float32)
        tbl_26 = 0.05 * jax.random.normal(jax.random.fold_in(_tk, 500 + 26), (12500, 16), jnp.float32)
        tbl_27 = 0.05 * jax.random.normal(jax.random.fold_in(_tk, 500 + 27), (125000, 16), jnp.float32)
        tbl_28 = 0.05 * jax.random.normal(jax.random.fold_in(_tk, 500 + 28), (1000, 16), jnp.float32)
        tbl_29 = 0.05 * jax.random.normal(jax.random.fold_in(_tk, 500 + 29), (1000, 16), jnp.float32)
        tbl_30 = 0.05 * jax.random.normal(jax.random.fold_in(_tk, 500 + 30), (1250, 16), jnp.float32)
        tbl_31 = 0.05 * jax.random.normal(jax.random.fold_in(_tk, 500 + 31), (12500, 16), jnp.float32)
        tbl_32 = 0.05 * jax.random.normal(jax.random.fold_in(_tk, 500 + 32), (1250, 16), jnp.float32)
        tbl_33 = 0.05 * jax.random.normal(jax.random.fold_in(_tk, 500 + 33), (1000, 16), jnp.float32)
        tbl_34 = 0.05 * jax.random.normal(jax.random.fold_in(_tk, 500 + 34), (12500, 16), jnp.float32)
        tbl_35 = 0.05 * jax.random.normal(jax.random.fold_in(_tk, 500 + 35), (1000, 16), jnp.float32)
        tbl_36 = 0.05 * jax.random.normal(jax.random.fold_in(_tk, 500 + 36), (1000, 16), jnp.float32)
        tbl_37 = 0.05 * jax.random.normal(jax.random.fold_in(_tk, 500 + 37), (12500, 16), jnp.float32)
        tbl_38 = 0.05 * jax.random.normal(jax.random.fold_in(_tk, 500 + 38), (125000, 16), jnp.float32)
        _rk = jax.random.fold_in(_tk, 7)
        W_top1 = 0.05 * jax.random.normal(jax.random.fold_in(_tk, 801), (400, 512), jnp.float32)
        W_top2 = 0.0441942 * jax.random.normal(jax.random.fold_in(_tk, 802), (512, 256), jnp.float32)
        W_top3 = 0.0625 * jax.random.normal(jax.random.fold_in(_tk, 803), (256, 1), jnp.float32)
        b_top1 = jnp.zeros((512,), jnp.float32)
        b_top2 = jnp.zeros((256,), jnp.float32)
        return (dense_ctx, ids, tbl_0, tbl_1, tbl_2, tbl_3, tbl_4, tbl_5, tbl_6, tbl_7, tbl_8, tbl_9, tbl_10, tbl_11, tbl_12, tbl_13, tbl_14, tbl_15, tbl_16, tbl_17, tbl_18, tbl_19, tbl_20, tbl_21, tbl_22, tbl_23, tbl_24, tbl_25, tbl_26, tbl_27, tbl_28, tbl_29, tbl_30, tbl_31, tbl_32, tbl_33, tbl_34, tbl_35, tbl_36, tbl_37, tbl_38, W_top1, b_top1, W_top2, b_top2, W_top3)
    dense_ctx, ids, tbl_0, tbl_1, tbl_2, tbl_3, tbl_4, tbl_5, tbl_6, tbl_7, tbl_8, tbl_9, tbl_10, tbl_11, tbl_12, tbl_13, tbl_14, tbl_15, tbl_16, tbl_17, tbl_18, tbl_19, tbl_20, tbl_21, tbl_22, tbl_23, tbl_24, tbl_25, tbl_26, tbl_27, tbl_28, tbl_29, tbl_30, tbl_31, tbl_32, tbl_33, tbl_34, tbl_35, tbl_36, tbl_37, tbl_38, W_top1, b_top1, W_top2, b_top2, W_top3 = _rec_inputs()

    def _L0_rec_setup():
        import jax, jax.numpy as jnp
        import numpy as np
        B, F0, D = (512, 39, 16)
        CIN = [128, 128, 128]

        def _cin_layer(X0, Xi, W, b):
            H = W.shape[0]
            F0_, Fi = (X0.shape[1], Xi.shape[1])
            Wr = W.reshape(H, F0_, Fi)
            return jnp.einsum('hjk,bjd,bkd->bhd', Wr, X0, Xi) + b[None, :, None]
        key = jax.random.key(seed)
        ks = jax.random.split(key, 4)
        x = jax.random.normal(ks[0], (B, F0, D), dtype=jnp.float32)
        fields = [F0] + CIN
        inp = {'embedded_features': x}
        for i in range(len(CIN)):
            cin = F0 * fields[i]
            cout = fields[i + 1]
            kw = jax.random.fold_in(ks[1], i)
            inp[f'W{i}'] = jax.random.normal(kw, (cout, cin), dtype=jnp.float32) / np.sqrt(cin)
            inp[f'b{i}'] = jnp.zeros((cout,), dtype=jnp.float32)
        return inp
    _L0_rec_all = _L0_rec_setup()
    _L0_rec_in = {k: v for k, v in _L0_rec_all.items() if k in ('W0', 'b0', 'W1', 'b1', 'W2', 'b2')}
    del _L0_rec_all
    return {'dense_ctx': dense_ctx, 'ids': ids, 'tbl_0': tbl_0, 'tbl_1': tbl_1, 'tbl_2': tbl_2, 'tbl_3': tbl_3, 'tbl_4': tbl_4, 'tbl_5': tbl_5, 'tbl_6': tbl_6, 'tbl_7': tbl_7, 'tbl_8': tbl_8, 'tbl_9': tbl_9, 'tbl_10': tbl_10, 'tbl_11': tbl_11, 'tbl_12': tbl_12, 'tbl_13': tbl_13, 'tbl_14': tbl_14, 'tbl_15': tbl_15, 'tbl_16': tbl_16, 'tbl_17': tbl_17, 'tbl_18': tbl_18, 'tbl_19': tbl_19, 'tbl_20': tbl_20, 'tbl_21': tbl_21, 'tbl_22': tbl_22, 'tbl_23': tbl_23, 'tbl_24': tbl_24, 'tbl_25': tbl_25, 'tbl_26': tbl_26, 'tbl_27': tbl_27, 'tbl_28': tbl_28, 'tbl_29': tbl_29, 'tbl_30': tbl_30, 'tbl_31': tbl_31, 'tbl_32': tbl_32, 'tbl_33': tbl_33, 'tbl_34': tbl_34, 'tbl_35': tbl_35, 'tbl_36': tbl_36, 'tbl_37': tbl_37, 'tbl_38': tbl_38, 'W_top1': W_top1, 'b_top1': b_top1, 'W_top2': W_top2, 'b_top2': b_top2, 'W_top3': W_top3, 'L0_rec_W0': _L0_rec_in['W0'], 'L0_rec_b0': _L0_rec_in['b0'], 'L0_rec_W1': _L0_rec_in['W1'], 'L0_rec_b1': _L0_rec_in['b1'], 'L0_rec_W2': _L0_rec_in['W2'], 'L0_rec_b2': _L0_rec_in['b2']}

def reference(dense_ctx, ids, tbl_0, tbl_1, tbl_2, tbl_3, tbl_4, tbl_5, tbl_6, tbl_7, tbl_8, tbl_9, tbl_10, tbl_11, tbl_12, tbl_13, tbl_14, tbl_15, tbl_16, tbl_17, tbl_18, tbl_19, tbl_20, tbl_21, tbl_22, tbl_23, tbl_24, tbl_25, tbl_26, tbl_27, tbl_28, tbl_29, tbl_30, tbl_31, tbl_32, tbl_33, tbl_34, tbl_35, tbl_36, tbl_37, tbl_38, W_top1, b_top1, W_top2, b_top2, W_top3, L0_rec_W0, L0_rec_b0, L0_rec_W1, L0_rec_b1, L0_rec_W2, L0_rec_b2):
    import jax
    import jax.numpy as jnp

    def _L0_rec_ref(embedded_features, W0, b0, W1, b1, W2, b2):
        import jax, jax.numpy as jnp
        import numpy as np
        B, F0, D = (512, 39, 16)
        CIN = [128, 128, 128]

        def _cin_layer(X0, Xi, W, b):
            H = W.shape[0]
            F0_, Fi = (X0.shape[1], Xi.shape[1])
            Wr = W.reshape(H, F0_, Fi)
            return jnp.einsum('hjk,bjd,bkd->bhd', Wr, X0, Xi) + b[None, :, None]
        X0 = embedded_features
        Ws = [(W0, b0), (W1, b1), (W2, b2)]
        Xi = X0
        res = []
        for W, b in Ws:
            Xi = _cin_layer(X0, Xi, W, b)
            res.append(Xi.sum(axis=2))
        return jnp.concatenate(res, axis=1)
    e = jnp.stack([tbl_0[ids[:, 0]], tbl_1[ids[:, 1]], tbl_2[ids[:, 2]], tbl_3[ids[:, 3]], tbl_4[ids[:, 4]], tbl_5[ids[:, 5]], tbl_6[ids[:, 6]], tbl_7[ids[:, 7]], tbl_8[ids[:, 8]], tbl_9[ids[:, 9]], tbl_10[ids[:, 10]], tbl_11[ids[:, 11]], tbl_12[ids[:, 12]], tbl_13[ids[:, 13]], tbl_14[ids[:, 14]], tbl_15[ids[:, 15]], tbl_16[ids[:, 16]], tbl_17[ids[:, 17]], tbl_18[ids[:, 18]], tbl_19[ids[:, 19]], tbl_20[ids[:, 20]], tbl_21[ids[:, 21]], tbl_22[ids[:, 22]], tbl_23[ids[:, 23]], tbl_24[ids[:, 24]], tbl_25[ids[:, 25]], tbl_26[ids[:, 26]], tbl_27[ids[:, 27]], tbl_28[ids[:, 28]], tbl_29[ids[:, 29]], tbl_30[ids[:, 30]], tbl_31[ids[:, 31]], tbl_32[ids[:, 32]], tbl_33[ids[:, 33]], tbl_34[ids[:, 34]], tbl_35[ids[:, 35]], tbl_36[ids[:, 36]], tbl_37[ids[:, 37]], tbl_38[ids[:, 38]]], axis=1)
    z = _L0_rec_ref(e, L0_rec_W0, L0_rec_b0, L0_rec_W1, L0_rec_b1, L0_rec_W2, L0_rec_b2)
    z = z.reshape(z.shape[0], -1)
    h = jnp.concatenate([z, dense_ctx], axis=1)
    h = jnp.maximum(h @ W_top1 + b_top1, 0.0)
    h = jnp.maximum(h @ W_top2 + b_top2, 0.0)
    y = h @ W_top3
    return y

_drawn_inputs = setup_inputs


def setup_inputs(seed=0):
    import zlib

    import numpy as np

    out = dict(_drawn_inputs(seed))
    spreads = {'b_top1': (0.0, 0.1),
     'b_top2': (0.0, 0.1),
     'L0_rec_b0': (0.0, 0.1),
     'L0_rec_b1': (0.0, 0.1),
     'L0_rec_b2': (0.0, 0.1)}
    factors = {'tbl_0': 8.0,
     'tbl_1': 5.809,
     'tbl_2': 5.017,
     'tbl_3': 6.897,
     'tbl_4': 8.0,
     'tbl_5': 8.0,
     'tbl_6': 8.0,
     'tbl_7': 7.049,
     'tbl_8': 8.0,
     'tbl_9': 8.0,
     'tbl_10': 8.0,
     'tbl_11': 6.708,
     'tbl_12': 8.0,
     'tbl_13': 8.0,
     'tbl_14': 4.37,
     'tbl_15': 5.467,
     'tbl_16': 8.0,
     'tbl_17': 8.0,
     'tbl_18': 8.0,
     'tbl_19': 5.748,
     'tbl_20': 7.059,
     'tbl_21': 8.0,
     'tbl_22': 8.0,
     'tbl_23': 8.0,
     'tbl_24': 8.0,
     'tbl_25': 7.242,
     'tbl_26': 6.091,
     'tbl_27': 8.0,
     'tbl_28': 8.0,
     'tbl_29': 8.0,
     'tbl_30': 6.425,
     'tbl_31': 6.483,
     'tbl_32': 8.0,
     'tbl_33': 6.364,
     'tbl_34': 8.0,
     'tbl_35': 7.574,
     'tbl_36': 8.0,
     'tbl_37': 6.643,
     'tbl_38': 8.0,
     'L0_rec_W0': 3.129}
    for name, (base, spread) in spreads.items():
        noise = np.random.default_rng([zlib.crc32(name.encode()), seed]).standard_normal(out[name].shape)
        drawn = base * np.exp(spread * noise) if base else spread * noise
        out[name] = jnp.asarray(drawn.astype(out[name].dtype))
    for name, factor in factors.items():
        out[name] = (out[name] * factor).astype(out[name].dtype)
    return out
```

```python
import concourse.bass as bass
from concourse import mybir
from contextlib import ExitStack

B, F, D, H = 1024, 39, 16, 128
BT = 128
T = B // BT
COLS = BT * D
N = 512
Q = COLS // N
JJ, KK = 8, 16
NG = (F + JJ - 1) // JJ
NM = H // KK
ND = 3
NT0 = (F // 2 + 1 + ND - 1) // ND
P0 = ND * F
ROWS = F + ND * NT0 - 1
HALF = 4
RING = 3
CI = 2 * (NG + 1)
ITEMS = Q * CI
L0_ITEM = 2
LEAD = 2
FS = F + 1
SB = BT // D
GROUPS = BT // SB
NP = GROUPS // 2
NX = (F * D + 127) // 128
XLAST = F * D - 128 * (NX - 1)
M1, M2 = 512, 256
C1, C2 = M1 // 128, M2 // 128


def hook_item(h):
    return 2 * h + 1


def items_made(t, i, last=False):
    gone = 2 if last and i >= ITEMS - CI + L0_ITEM + 2 else 0
    return LEAD + ITEMS * t + i + 1 - gone


def is_l0(i):
    return i % CI in (L0_ITEM, L0_ITEM + 1)


def skipped(i, last):
    return last and i >= ITEMS - CI and is_l0(i)


def build(nc, ids, tables, dense_t, w0a, w0b, b0, w1, b1, w2, b2, wt1, wt1d, bt1, wt2, bt2, wt3, y_out):
    fp32 = mybir.dt.float32
    i32 = mybir.dt.int32
    ALU = mybir.AluOpType
    ACT = mybir.ActivationFunctionType
    AX = mybir.AxisListType

    x0_rows = nc.dram_tensor("x0_rows", [T, ROWS, COLS], fp32)

    x1_rows = nc.dram_tensor("x1_rows", [T, Q, H, N], fp32)

    ctx = ExitStack()
    with ctx:
        def sb(name, shape, dt=fp32):
            return ctx.enter_context(nc.sbuf_tensor(name, shape, dt))

        def pb(name, shape):
            return ctx.enter_context(nc.psum_tensor(name, shape, fp32))

        def sem(name):
            return ctx.enter_context(nc.semaphore(name))

        w0_sb = sb("w0_sb", [P0, NT0, H])
        w1_sb = sb("w1_sb", [128, NG * NM, H])
        w2_sb = sb("w2_sb", [H, F, H])
        wt1_sb = sb("wt1_sb", [H, 3, M1])
        wt1d_sb = sb("wt1d_sb", [D, M1])
        wt2_sb = sb("wt2_sb", [128, C1, M2])
        wt3_sb = sb("wt3_sb", [128, C2])
        bias = sb("bias", [128, 4 + C1 + C2])
        eye = sb("eye", [128, 128])
        ids_sb = sb("ids_sb", [BT, F], i32)
        emb = sb("emb", [BT, F, D])
        x0_turned = sb("x0_turned", [128, NX, BT])
        x0_cols = sb("x0_cols", [F, COLS])
        x2 = sb("x2", [H, COLS])
        g_sb = sb("g_sb", [H, FS, BT])
        z1_parts = sb("z1_parts", [H, Q, BT])
        z1 = sb("z1", [H, BT])
        z3 = sb("z3", [H, BT])
        dense_sb = sb("dense_sb", [D, BT])
        h1 = sb("h1", [128, C1, BT])
        h2 = sb("h2", [128, C2, BT])
        y_sb = sb("y_sb", [1, BT])
        l0_left = sb("l0_left", [P0, N])
        l0_right = sb("l0_right", [P0, NT0, N])
        l1_left = sb("l1_left", [128, 2, NG, N])
        l1_right = sb("l1_right", [128, 2, NM, N])
        x1 = sb("x1", [H, 2, N])
        products = sb("products", [128, RING, HALF, N])
        x2_turned = sb("x2_turned", [128, 2, 2, H])
        x0_diag = sb("x0_diag", [128, 2, 2, FS, SB])

        x1_ps = pb("x1_ps", [H, N])
        x2_ps = pb("x2_ps", [H, 2, N])
        x2_turn_ps = pb("x2_turn_ps", [128, N])
        x0_turn_ps = pb("x0_turn_ps", [128, N])
        g_ps = pb("g_ps", [128, 2, N])
        mlp_ps = pb("mlp_ps", [128, N])

        weights_loaded = sem("weights_loaded")
        eye_made = sem("eye_made")
        mask_made = sem("mask_made")
        w0_folded = sem("w0_folded")
        b2_scaled = sem("b2_scaled")
        first_ids_loaded = sem("first_ids_loaded")
        ids_loaded = sem("ids_loaded")
        emb_gathered = sem("emb_gathered")
        emb_turned = sem("emb_turned")
        x0_kept = sem("x0_kept")
        x0_stored = sem("x0_stored")
        x0_cols_loaded = sem("x0_cols_loaded")
        dense_loaded = sem("dense_loaded")
        l0_loaded = sem("l0_loaded")
        left_loaded = [sem(f"left_loaded{s}") for s in range(2)]
        right_loaded = [sem(f"right_loaded{s}") for s in range(2)]
        products_made = sem("products_made")
        products_used = sem("products_used")
        x1_kept = sem("x1_kept")
        x2_kept = sem("x2_kept")
        x1_stored = [sem(f"x1_stored{s}") for s in range(2)]
        x1_summed = sem("x1_summed")
        z1_made = sem("z1_made")
        pair_turned = sem("pair_turned")
        x2_turned_kept = sem("x2_turned_kept")
        diag_made = sem("diag_made")
        g_made = sem("g_made")
        g_kept = sem("g_kept")
        z3_made = sem("z3_made")
        z3_kept = sem("z3_kept")
        h1_made = sem("h1_made")
        h1_kept = sem("h1_kept")
        h2_made = sem("h2_made")
        h2_kept = sem("h2_kept")
        y_made = sem("y_made")
        y_kept = sem("y_kept")
        y_stored = sem("y_stored")

        w0b_sb = x2[0:P0, 0:NT0 * H].rearrange("p (t h) -> p t h", t=NT0)

        block = ctx.enter_context(nc.Block())

        @block.sync
        def _(sp):
            def load_l0(t, q):
                cols = slice(q * N, (q + 1) * N)
                for delta in range(ND):
                    rows = slice(F * delta, F * (delta + 1))
                    sp.dma_start(l0_left[rows, :].unsqueeze(1),
                                 x0_rows[bass.ds(t, 1), 0:F, cols].rearrange("o f n -> f o n")).then_inc(l0_loaded, 16)
                    src = x0_rows[bass.ds(t, 1), delta:delta + 1, cols]
                    sp.dma_start(l0_right[rows, :, :],
                                 bass.AP(x0_rows, src.offset, [[COLS, F], [ND * COLS, NT0], [1, N]])).then_inc(l0_loaded, 16)

            def load_left(t, q):
                for jj in range(JJ):
                    src = x0_rows[bass.ds(t, 1), jj:jj + 1, q * N:(q + 1) * N]
                    sp.dma_start(l1_left[KK * jj:KK * (jj + 1), q % 2, :, :],
                                 bass.AP(x0_rows, src.offset, [[0, KK], [JJ * COLS, NG], [1, N]])
                                 ).then_inc(left_loaded[q % 2], 16)

            def load_right(t, q, stored):
                s = q % 2
                sp.dma_start(x1_rows[bass.ds(t, 1), q, :, :].rearrange("o h n -> h o n"), x1[:, s, :].unsqueeze(1)).then_inc(x1_stored[s], 16)
                sp.wait_ge(x1_stored[s], stored)
                for jj in range(JJ):
                    sp.dma_start(l1_right[KK * jj:KK * (jj + 1), s, :, :],
                                 x1_rows[bass.ds(t, 1), q, :, :].rearrange("o (m k) n -> (o k) m n", k=KK)
                                 ).then_inc(right_loaded[s], 16)

            def store_x0(t):
                sp.wait_ge(x0_kept, t + 1)
                wrap = ROWS - F
                full, rest = wrap * D // 128, wrap * D % 128
                for rows, g0, ng, at in ((128, 0, NX - 1, 0), (XLAST, NX - 1, 1, 0),
                                         (128, 0, full, F), (rest, full, 1, F)):
                    dst = x0_rows[bass.ds(t, 1), at:at + 1, 0:BT]
                    sp.dma_start(
                        bass.AP(x0_rows, dst.offset + g0 * 128 * BT, [[BT, rows], [128 * BT, ng], [1, BT]]),
                        x0_turned[0:rows, g0:g0 + ng, :],
                    ).then_inc(x0_stored, 16)

            for dst, src in ((w0_sb[:, :, :], w0a), (w0b_sb, w0b), (bias[:, 0:1], b0), (bias[:, 1:2], b1),
                             (bias[:, 2:3], b2), (bias[:, 4:4 + C1], bt1), (bias[:, 4 + C1:4 + C1 + C2], bt2),
                             (w1_sb[:, :, :], w1), (w2_sb[:, :, :], w2), (wt1_sb[:, :, :], wt1),
                             (wt1d_sb[:, :], wt1d), (wt2_sb[:, :, :], wt2), (wt3_sb[:, :], wt3)):
                sp.dma_start(dst, src).then_inc(weights_loaded, 16)

            store_x0(0)
            sp.wait_ge(x0_stored, 64)
            load_l0(0, 0)
            load_left(0, 0)
            sp.wait_ge(products_made, LEAD)
            load_l0(0, 1)
            sp.wait_ge(x1_kept, 1)
            load_right(0, 0, 16)

            def tile(t, first=False, last=False):
                for q in range(Q):
                    i = q * CI
                    nt, nq = (t, q + 1) if q + 1 < Q else (t + 1, 0)
                    if not (last and q == Q - 1):
                        if not (first and q == 0):
                            sp.wait_ge(products_made, items_made(t, i - 1))
                        load_left(nt, nq)
                        nnt, nnq = (t, q + 2) if q + 2 < Q else (t + 1, q + 2 - Q)
                        if not (last and q + 2 >= Q):
                            sp.wait_ge(products_made, items_made(t, i + L0_ITEM + 1))
                            load_l0(nnt, nnq)
                        sp.wait_ge(x1_kept, Q * t + q + 2)
                        if q == 2 and not first:
                            sp.wait_ge(h1_made, t)
                        load_right(nt, nq, 16 * (2 * nt + nq // 2 + 1))
                    if q == 0 and not last:
                        store_x0(t + 1)
                    if q == 2:
                        sp.dma_start(x0_cols[:, :].unsqueeze(1),
                                     x0_rows[bass.ds(t, 1), 0:F, :].rearrange("o f n -> f o n")
                                     ).then_inc(x0_cols_loaded, 16)
                        sp.dma_start(dense_sb[:, :], dense_t[:, bass.ds(t * BT, BT)]).then_inc(dense_loaded, 16)
                    if q == 3 and not first:
                        sp.wait_ge(y_kept, t)
                        sp.dma_start(y_out[:, bass.ds((t - 1) * BT, BT)], y_sb[:, :]).then_inc(y_stored, 16)

            tile(0, first=True)
            with sp.Fori(1, T - 1) as t:
                tile(t)
            tile(T - 1, last=True)
            sp.wait_ge(y_kept, T)
            sp.dma_start(y_out[:, (T - 1) * BT:], y_sb[:, :]).then_inc(y_stored, 16)
            sp.wait_ge(y_stored, 16 * T)

        @block.gpsimd
        def _(pool):
            nc.gpsimd.memset(eye[:, :], 0.0).then_inc(eye_made, 1)
            pool.wait_ge(eye_made, 1)
            nc.gpsimd.affine_select(out=eye[:, :], in_=eye[:, :], compare_op=ALU.not_equal, fill=1.0, base=0,
                                    pattern=[[-1, 128]], channel_multiplier=1).then_inc(eye_made, 1)

            def gather(row, arrived, semaphore):
                pool.dma_start(ids_sb[:, :], ids[bass.ds(row, BT), :]).then_inc(semaphore, 16)
                pool.wait_ge(eye_made, 2)
                pool.wait_ge(semaphore, arrived)
                for f in range(F):
                    pool.indirect_dma_start(
                        out=emb[:, f, :], out_offset=None, in_=tables[f],
                        in_offset=bass.IndirectOffsetOnAxis(ap=ids_sb[:, f:f + 1], axis=0),
                    ).then_inc(emb_gathered, 16)

            gather(0, 16, first_ids_loaded)
            with pool.Fori(16, 16 * (T - 1) + 1, 16) as t16:
                pool.wait_ge(emb_turned, t16 // 16)
                gather(t16 * (BT // 16), t16, ids_loaded)

        @block.scalar
        def _(act):
            def keep_x0(t):
                act.wait_ge(emb_turned, t + 1)
                if not isinstance(t, int) or t > 0:
                    act.wait_ge(x0_stored, 64 * t)
                nc.scalar.activation(x0_turned[:, 0:NX - 1, :], g_ps[:, 0, :].rearrange("p (g b) -> p g b", b=BT), ACT.Copy)
                nc.scalar.activation(x0_turned[0:XLAST, NX - 1, :], g_ps[0:XLAST, 1, 0:BT], ACT.Copy).then_inc(x0_kept, 1)

            def keep_x1(t, q, used, early=False):
                act.wait_ge(products_used, used)
                if not early:
                    act.wait_ge(x1_stored[q % 2], 16 * (2 * t + q // 2))
                    act.wait_ge(x1_summed, Q * t + q - 1)
                nc.scalar.activation(x1[:, q % 2, :], x1_ps[:, :], ACT.Identity, bias=bias[:, 0:1]).then_inc(x1_kept, 1)

            def keep_x2(t, q, last=False):
                act.wait_ge(products_used, items_made(t, q * CI + CI - 1, last))
                nc.scalar.activation(x2[:, q * N:(q + 1) * N], x2_ps[:, q % 2, :], ACT.Identity,
                                     bias=bias[:, 1:2]).then_inc(x2_kept, 1)

            def tail(n, h):
                if 1 <= h <= NP:
                    p = h - 1
                    act.wait_ge(pair_turned, NP * n + p + 1)
                    nc.scalar.activation(x2_turned[:, p % 2, :, :], x2_turn_ps[:, 0:2 * H].rearrange("p (i h) -> p i h", i=2),
                                         ACT.Copy).then_inc(x2_turned_kept, 1)
                if 2 <= h <= NP + 1:
                    p = h - 2
                    act.wait_ge(g_made, NP * n + p + 1)
                    nc.scalar.activation(
                        g_sb[:, :, :].rearrange("k j (b c) -> k c j b", c=GROUPS)[:, 2 * p:2 * p + 2, :, :],
                        g_ps[:, :, 0:FS * SB].rearrange("k i (j b) -> k i j b", b=SB), ACT.Copy).then_inc(g_kept, 1)
                if h == NP + 2:
                    act.wait_ge(z3_made, n + 1)
                    nc.scalar.activation(z3[:, :], mlp_ps[:, 0:BT], ACT.Identity, bias=bias[:, 3:4]).then_inc(z3_kept, 1)
                if h == NP + 3:
                    act.wait_ge(h1_made, n + 1)
                    for m in range(C1):
                        last = nc.scalar.activation(h1[:, m, :], mlp_ps[:, m * BT:(m + 1) * BT], ACT.Relu,
                                                    bias=bias[:, 4 + m:5 + m])
                    last.then_inc(h1_kept, 1)
                if h == NP + 4:
                    act.wait_ge(h2_made, n + 1)
                    for m in range(C2):
                        last = nc.scalar.activation(h2[:, m, :], mlp_ps[:, m * BT:(m + 1) * BT], ACT.Relu,
                                                    bias=bias[:, 4 + C1 + m:5 + C1 + m])
                    last.then_inc(h2_kept, 1)
                if h == NP + 5:
                    act.wait_ge(y_made, n + 1)
                    nc.scalar.activation(y_sb[:, :], mlp_ps[0:1, 0:BT], ACT.Copy).then_inc(y_kept, 1)
                if h == ITEMS // 2 - 1:
                    act.wait_ge(y_stored, 16 * (n + 1))

            act.wait_ge(b2_scaled, 1)
            keep_x0(0)
            keep_x1(0, 0, LEAD, early=True)

            def tile(t, first=False, last=False):
                for i in range(ITEMS):
                    q = i // CI
                    if i % CI == L0_ITEM + 1 and not skipped(i, last):
                        if q + 1 < Q:
                            if q == 1 and not last:
                                act.wait_ge(x0_stored, 64 * (t + 2))
                            keep_x1(t, q + 1, items_made(t, i, last), early=first and q == 0)
                        else:
                            keep_x1(t + 1, 0, items_made(t, i, last))
                    if i % 2 == 1:
                        h = i // 2
                        if h == 0 and not last:
                            keep_x0(t + 1)
                        if not first:
                            tail(t - 1, h)
                        if h == NP + 1:
                            keep_x2(t, 0, last)
                    if i % CI == CI - 1 and q > 0:
                        keep_x2(t, q, last)

            tile(0, first=True)
            with act.Fori(1, T - 1) as t:
                tile(t)
            tile(T - 1, last=True)
            for h in range(1, NP + 6):
                tail(T - 1, h)

        @block.vector
        def _(dve):
            dve.wait_ge(weights_loaded, 16 * 13)
            nc.vector.tensor_tensor(w0_sb[:, :, :], w0_sb[:, :, :], w0b_sb, ALU.add).then_inc(w0_folded, 1)
            nc.vector.tensor_scalar(bias[:, 3:4], bias[:, 2:3], float(D), None, ALU.mult).then_inc(b2_scaled, 1)
            dve.wait_ge(eye_made, 2)
            nc.vector.tensor_reduce(x0_diag[:, 0, 0, F, :], eye[:, :].rearrange("p (d b) -> p b d", b=SB),
                                    AX.X, ALU.add).then_inc(mask_made, 1)
            dve.wait_ge(mask_made, 1)
            for s, i in ((0, 1), (1, 0), (1, 1)):
                nc.vector.tensor_copy(x0_diag[:, s, i, F, :], x0_diag[:, 0, 0, F, :]).then_inc(mask_made, 1)
            dve.wait_ge(mask_made, 4)

            def multiply_l0(t, q, half, slot):
                c = Q * t + q
                n = min(HALF, NT0 - HALF * half)
                if half == 0:
                    dve.wait_ge(l0_loaded, 16 * 2 * ND * (c + 1))
                nc.vector.tensor_tensor(products[0:P0, slot, 0:n, :],
                                        l0_left[:, :].unsqueeze(1).broadcast_to([P0, n, N]),
                                        l0_right[:, HALF * half:HALF * half + n, :], ALU.mult).then_inc(products_made, 1)

            def multiply_l1(t, q, g, half, slot):
                if g == 0 and half == 0:
                    dve.wait_ge(left_loaded[q % 2], 16 * JJ * (2 * t + q // 2 + 1))
                    dve.wait_ge(right_loaded[q % 2], 16 * JJ * (2 * t + q // 2 + 1))
                nc.vector.tensor_tensor(products[:, slot, :, :],
                                        l1_left[:, q % 2, g, :].unsqueeze(1).broadcast_to([128, HALF, N]),
                                        l1_right[:, q % 2, HALF * half:HALF * (half + 1), :], ALU.mult).then_inc(products_made, 1)

            def tail(n, h):
                if 1 <= h <= NP:
                    p = h - 1
                    dve.wait_ge(pair_turned, NP * n + p + 1)
                    for i in range(2):
                        last = nc.vector.tensor_tensor(
                            x0_diag[:, p % 2, i, 0:F, :],
                            x0_turn_ps[:, i * F:(i + 1) * F].unsqueeze(2).broadcast_to([128, F, SB]),
                            x0_diag[:, p % 2, i, F, :].unsqueeze(1).broadcast_to([128, F, SB]), ALU.mult)
                    last.then_inc(diag_made, 1)

            def sum_x1(t, q):
                dve.wait_ge(x1_kept, Q * t + q + 1)
                nc.vector.tensor_reduce(z1_parts[:, q, :], x1[:, q % 2, :].rearrange("h (d b) -> h b d", b=BT),
                                        AX.X, ALU.add).then_inc(x1_summed, 1)

            def sum_z1(t):
                dve.wait_ge(x1_summed, Q * t + Q)
                if not isinstance(t, int) or t > 0:
                    dve.wait_ge(h1_made, t)
                nc.vector.tensor_reduce(z1[:, :], z1_parts[:, :, :].rearrange("h q b -> h b q"),
                                        AX.X, ALU.add).then_inc(z1_made, 1)

            multiply_l0(0, 0, 0, -2 % RING)
            multiply_l0(0, 0, 1, -1 % RING)

            def tile(t, first=False, last=False):
                for i in range(ITEMS):
                    q, r = i // CI, i % CI
                    if not skipped(i, last):
                        back = i - RING
                        if skipped(back, last):
                            back -= RING
                        if not (first and i < RING - LEAD):
                            dve.wait_ge(products_used, items_made(t, back, last))
                        if is_l0(i):
                            nt, nq = (t, q + 1) if q + 1 < Q else (t + 1, 0)
                            multiply_l0(nt, nq, r - L0_ITEM, i % RING)
                        else:
                            g = 0 if r < L0_ITEM else (r - L0_ITEM) // 2
                            multiply_l1(t, q, g, r % 2, i % RING)
                    if i % 2 == 1 and not first:
                        tail(t - 1, (i - RING) // 2)
                    if first and i == 1:
                        sum_x1(0, 0)
                    if r == L0_ITEM + 1 + RING + 1 and not (last and q == Q - 1):
                        if q + 1 < Q:
                            sum_x1(t, q + 1)
                        else:
                            sum_x1(t + 1, 0)
                    if q == Q - 2 and r == CI - 2:
                        sum_z1(t)

            tile(0, first=True)
            with dve.Fori(1, T - 1) as t:
                tile(t)
            tile(T - 1, last=True)
            for h in range(1, NP + 1):
                tail(T - 1, h)

        @block.tensor
        def _(pe):
            mm = nc.tensor.matmul

            def turn_emb(t):
                pe.wait_ge(emb_gathered, 16 * F * (t + 1))
                flat = emb[:, :, :].rearrange("b f d -> b (f d)")
                for g in range(NX):
                    rows = XLAST if g == NX - 1 else 128
                    last = nc.tensor.transpose(g_ps[0:rows, g // 4, (g % 4) * BT:(g % 4 + 1) * BT],
                                               flat[:, 128 * g:128 * g + rows], eye[:, :])
                last.then_inc(emb_turned, 1)

            def layer0(t, q, half, slot, made):
                c = Q * t + q
                pe.wait_ge(products_made, made)
                if half == 0 and not (isinstance(c, int) and c < 1):
                    pe.wait_ge(x1_kept, c)
                n = min(HALF, NT0 - HALF * half)
                for k in range(n):
                    at = HALF * half + k
                    last = mm(x1_ps[:, :], w0_sb[:, at, :], products[0:P0, slot, k, :],
                              start=at == 0, stop=at == NT0 - 1)
                last.then_inc(products_used, 1)

            def layer1(t, q, g, half, slot, made):
                c = Q * t + q
                pe.wait_ge(products_made, made)
                if g == 0 and half == 0 and not (isinstance(c, int) and c < 2):
                    pe.wait_ge(x2_kept, c - 1)
                for k in range(HALF):
                    at = NM * g + HALF * half + k
                    last = mm(x2_ps[:, q % 2, :], w1_sb[:, at, :], products[:, slot, k, :],
                              start=at == 0, stop=at == NG * NM - 1)
                last.then_inc(products_used, 1)

            def tail(n, h):
                if 1 <= h <= NP:
                    p = h - 1
                    if p == 0:
                        pe.wait_ge(x2_kept, Q * (n + 1))
                        pe.wait_ge(x0_cols_loaded, 16 * (n + 1))
                    else:
                        pe.wait_ge(x2_turned_kept, NP * n + p)
                        pe.wait_ge(diag_made, NP * n + p)
                    for i in range(2):
                        nc.tensor.transpose(x2_turn_ps[:, i * H:(i + 1) * H], x2[:, 2 * p + i::GROUPS], eye[:, :])
                    for i in range(2):
                        last = nc.tensor.transpose(x0_turn_ps[:, i * F:(i + 1) * F],
                                                   x0_cols[:, 2 * p + i::GROUPS], eye[0:F, 0:F])
                    last.then_inc(pair_turned, 1)
                if 2 <= h <= NP + 1:
                    p = h - 2
                    pe.wait_ge(x2_turned_kept, NP * n + p + 1)
                    pe.wait_ge(diag_made, NP * n + p + 1)
                    if p > 0:
                        pe.wait_ge(g_kept, NP * n + p)
                    for i in range(2):
                        last = mm(g_ps[:, i, 0:FS * SB], x2_turned[:, p % 2, i, :],
                                  x0_diag[:, p % 2, i, :, :].rearrange("p j b -> p (j b)"), start=True, stop=True)
                    last.then_inc(g_made, 1)
                if h == NP + 2:
                    pe.wait_ge(g_kept, NP * (n + 1))
                    for j in range(F):
                        last = mm(mlp_ps[:, 0:BT], w2_sb[:, j, :], g_sb[:, j, :], start=j == 0, stop=j == F - 1)
                    last.then_inc(z3_made, 1)
                if h == NP + 3:
                    pe.wait_ge(z3_kept, n + 1)
                    pe.wait_ge(z1_made, n + 1)
                    pe.wait_ge(dense_loaded, 16 * (n + 1))
                    for m in range(C1):
                        out = mlp_ps[:, m * BT:(m + 1) * BT]
                        cols = slice(128 * m, 128 * (m + 1))
                        for k, z in enumerate((z1[:, :], g_sb[:, F, :], z3[:, :])):
                            mm(out, wt1_sb[:, k, cols], z, start=k == 0, stop=False)
                        last = mm(out, wt1d_sb[:, cols], dense_sb[:, :], start=False, stop=True)
                    last.then_inc(h1_made, 1)
                if h == NP + 4:
                    pe.wait_ge(h1_kept, n + 1)
                    for m in range(C2):
                        for k in range(C1):
                            last = mm(mlp_ps[:, m * BT:(m + 1) * BT], wt2_sb[:, k, 128 * m:128 * (m + 1)], h1[:, k, :],
                                      start=k == 0, stop=k == C1 - 1)
                    last.then_inc(h2_made, 1)
                if h == NP + 5:
                    pe.wait_ge(h2_kept, n + 1)
                    for k in range(C2):
                        last = mm(mlp_ps[0:1, 0:BT], wt3_sb[:, k:k + 1], h2[:, k, :], start=k == 0, stop=k == C2 - 1)
                    last.then_inc(y_made, 1)
                if h == NP + 6:
                    pe.wait_ge(y_kept, n + 1)

            pe.wait_ge(eye_made, 2)
            turn_emb(0)
            pe.wait_ge(w0_folded, 1)
            layer0(0, 0, 0, -2 % RING, 1)
            layer0(0, 0, 1, -1 % RING, 2)

            def tile(t, first=False, last=False):
                for i in range(ITEMS):
                    q, r = i // CI, i % CI
                    made = items_made(t, i, last)
                    if not skipped(i, last):
                        if is_l0(i):
                            nt, nq = (t, q + 1) if q + 1 < Q else (t + 1, 0)
                            layer0(nt, nq, r - L0_ITEM, i % RING, made)
                        else:
                            g = 0 if r < L0_ITEM else (r - L0_ITEM) // 2
                            layer1(t, q, g, r % 2, i % RING, made)
                    if i % 2 == 1:
                        h = i // 2
                        if h == 0 and not last:
                            turn_emb(t + 1)
                        if h == 1 and not last:
                            pe.wait_ge(x0_kept, t + 2)
                        if not first:
                            tail(t - 1, h)

            tile(0, first=True)
            with pe.Fori(1, T - 1) as t:
                tile(t)
            tile(T - 1, last=True)
            for h in range(1, NP + 6):
                tail(T - 1, h)


def kernel(**inputs):
    import numpy as np
    import concourse.bacc as bacc
    from concourse.bass_utils import run_bass_kernel_spmd

    W0 = np.asarray(inputs["L0_rec_W0"]).reshape(H, F, F)
    W1 = np.asarray(inputs["L0_rec_W1"]).reshape(H, F, H)
    W2 = np.asarray(inputs["L0_rec_W2"]).reshape(H, F, H)
    Wt1 = np.asarray(inputs["W_top1"])
    Wt2 = np.asarray(inputs["W_top2"])

    j = np.arange(F)[None, :, None]
    delta = np.arange(NT0)[None, None, :] * ND + np.arange(ND)[:, None, None]
    k = (j + delta) % F
    j = np.broadcast_to(j, k.shape)
    w0a = np.zeros((ND, F, NT0, H), W0.dtype)
    w0b = np.zeros((ND, F, NT0, H), W0.dtype)
    once = np.broadcast_to(delta <= F // 2, k.shape)
    both = once & np.broadcast_to(delta > 0, k.shape)
    w0a[once] = W0[:, j[once], k[once]].T
    w0b[both] = W0[:, k[both], j[both]].T

    w1 = np.zeros((H, NG * JJ, H), W1.dtype)
    w1[:, :F] = W1
    w1 = w1.reshape(H, NG, JJ, NM, KK).transpose(2, 4, 1, 3, 0).reshape(128, NG * NM, H)

    arrays = {
        "ids": np.asarray(inputs["ids"]),
        "dense_t": np.asarray(inputs["dense_ctx"]).T,
        "w0a": w0a.reshape(P0, NT0, H),
        "w0b": w0b.reshape(P0, NT0, H),
        "b0": np.asarray(inputs["L0_rec_b0"]).reshape(H, 1),
        "w1": w1,
        "b1": np.asarray(inputs["L0_rec_b1"]).reshape(H, 1),
        "w2": W2.transpose(2, 1, 0),
        "b2": np.asarray(inputs["L0_rec_b2"]).reshape(H, 1),
        "wt1": Wt1[:3 * H].reshape(3, H, M1).transpose(1, 0, 2),
        "wt1d": Wt1[3 * H:],
        "bt1": np.asarray(inputs["b_top1"]).reshape(C1, 128).T,
        "wt2": Wt2.reshape(C1, 128, M2).transpose(1, 0, 2),
        "bt2": np.asarray(inputs["b_top2"]).reshape(C2, 128).T,
        "wt3": np.asarray(inputs["W_top3"]).reshape(C2, 128).T,
    }
    for f in range(F):
        arrays[f"tbl_{f}"] = np.asarray(inputs[f"tbl_{f}"])

    nc = bacc.Bacc("TRN2", target_bir_lowering=False, num_devices=1)
    aps = {}
    for name in arrays:
        arrays[name] = np.ascontiguousarray(arrays[name])
        aps[name] = nc.dram_tensor(f"in_{name}", arrays[name].shape, mybir.dt.from_np(arrays[name].dtype),
                                   kind="ExternalInput").ap()
    y_out = nc.dram_tensor("out_y", (1, B), mybir.dt.float32, kind="ExternalOutput").ap()
    build(nc, aps["ids"], [aps[f"tbl_{f}"] for f in range(F)], *[aps[n] for n in (
        "dense_t", "w0a", "w0b", "b0", "w1", "b1", "w2", "b2", "wt1", "wt1d", "bt1", "wt2", "bt2", "wt3")], y_out)
    r = run_bass_kernel_spmd(nc, [{f"in_{name}": a for name, a in arrays.items()}], core_ids=[0])
    return r.results[0]["out_y"].reshape(B, 1)
```

```python
import concourse.bass as bass
from concourse import mybir
from contextlib import ExitStack

B, F, D, H = 1024, 39, 16, 128
BT = 128
T = B // BT
COLS = BT * D
N = 512
Q = COLS // N
JJ, KK = 8, 16
NG = (F + JJ - 1) // JJ
NM = H // KK
ND = 3
NT0 = (F // 2 + 1 + ND - 1) // ND
P0 = ND * F
ROWS = F + ND * NT0 - 1
HALF = 4
RING = 3
SPLIT = 2
CI = 2 * (NG + 1)
ITEMS = Q * CI
L0_ITEMS = 2
LG = (3, 2)
LEAD = L0_ITEMS
FIRST = (-CI, -CI + 1)
FS = F + 1
SB = BT // D
GROUPS = BT // SB
NP = GROUPS // 2
NX = (F * D + 127) // 128
XLAST = F * D - 128 * (NX - 1)
EVERY = 3
TURN = [1 + EVERY * p for p in range(NP)]
CONTRACT = [m + 2 for m in TURN]
L2 = [CONTRACT[-1] + 2 + n for n in range(12)]
MLP1 = [L2[-1] + 2, L2[-1] + 3]
MLP2, MLP3, END = (MLP1[-1] + 2 * n for n in range(1, 4))
SUM_Z1 = MLP1[-1] + RING + 1
TURN_EMB, FIRST_TURN_EMB = TURN[0], 6
WARM = 6
KEEP_X2 = TURN[-1] + 1
M1, M2 = 512, 256
C1, C2 = M1 // 128, M2 // 128


def items_made(t, i, last=False):
    if isinstance(t, int) and t == 0 and i < 0:
        return i - FIRST[0] + 1
    gone = L0_ITEMS if last and i >= ITEMS - CI + L0_ITEMS else 0
    return LEAD + ITEMS * t + i + 1 - gone


def is_l0(i):
    return i % CI < L0_ITEMS


def skipped(i, last):
    return last and i >= ITEMS - CI and is_l0(i)


def slot_free(t, i, slots, last=False):
    if isinstance(t, int) and t == 0 and i < slots:
        return i + 1 if 0 <= i < LEAD else None
    back = i - slots
    while skipped(back, last):
        back -= slots
    return items_made(t, back, last)


def tiles_of(i):
    n = NT0 - HALF if i % CI == 1 else HALF
    return n, n - SPLIT


def l1_item(i):
    return divmod(i % CI - L0_ITEMS, NG)


def build(nc, ids, tables, dense_t, w0a, w0b, b0, w1, w1s, b1, w2, b2, wt1, wt1d, bt1, wt2, bt2, wt3, y_out):
    fp32 = mybir.dt.float32
    fp32r = mybir.dt.float32r
    i32 = mybir.dt.int32
    ALU = mybir.AluOpType
    ACT = mybir.ActivationFunctionType
    AX = mybir.AxisListType

    x0_rows = nc.dram_tensor("x0_rows", [T, ROWS, COLS], fp32)

    x1_rows = nc.dram_tensor("x1_rows", [T, Q, H, N], fp32)

    ctx = ExitStack()
    with ctx:
        def sb(name, shape, dt=fp32):
            return ctx.enter_context(nc.sbuf_tensor(name, shape, dt))

        def pb(name, shape):
            return ctx.enter_context(nc.psum_tensor(name, shape, fp32))

        def sem(name):
            return ctx.enter_context(nc.semaphore(name))

        w0_sb = sb("w0_sb", [P0, NT0 - 2 * SPLIT, H])
        w0_hi = sb("w0_hi", [P0, 2 * SPLIT, H], fp32r)
        w0_lo = sb("w0_lo", [P0, 2 * SPLIT, H], fp32r)
        w1_sb = sb("w1_sb", [128, 2 * NG * (HALF - SPLIT), H])
        w1_hi = sb("w1_hi", [128, 2 * NG * SPLIT, H], fp32r)
        w1_lo = sb("w1_lo", [128, 2 * NG * SPLIT, H], fp32r)
        w2_sb = sb("w2_sb", [H, F, H])
        wt1_sb = sb("wt1_sb", [H, 3, M1])
        wt2_sb = sb("wt2_sb", [128, C1, M2])
        wt3_sb = sb("wt3_sb", [128, C2])
        bias = sb("bias", [128, 4 + C1 + C2])
        eye = sb("eye", [128, 128])
        ids_sb = sb("ids_sb", [BT, F], i32)
        emb = sb("emb", [BT, F, D])
        x0_turned = sb("x0_turned", [128, NX, BT])
        shared = sb("shared", [128, COLS])
        x2 = sb("x2", [H, COLS])
        g_sb = sb("g_sb", [H, FS, BT])
        z1_parts = sb("z1_parts", [H, Q, BT])
        z1 = sb("z1", [H, BT])
        z3 = sb("z3", [H, BT])
        h1 = sb("h1", [128, C1, BT])
        h2 = sb("h2", [128, C2, BT])
        y_sb = sb("y_sb", [1, BT])
        l0_left = sb("l0_left", [P0, N])
        l0_right = sb("l0_right", [P0, NT0, N])
        l1_left = sb("l1_left", [128, NG, N])
        l1_right = sb("l1_right", [128, NM, N])
        x1 = sb("x1", [H, 2, N])
        products = sb("products", [128, RING, HALF, N])
        products_hi = sb("products_hi", [128, 2, SPLIT, N], fp32r)
        products_lo = sb("products_lo", [128, 2, SPLIT, N], fp32r)
        x2_turned = sb("x2_turned", [128, 2, 2, H])
        x0_diag = sb("x0_diag", [128, 2, 2, FS, SB])

        x1_ps = pb("x1_ps", [H, N])
        x2_ps = pb("x2_ps", [H, 2, N])
        turn_ps = pb("turn_ps", [128, N])
        g_ps = pb("g_ps", [128, 2, N])
        mlp_ps = pb("mlp_ps", [128, N])

        weights_loaded = sem("weights_loaded")
        eye_made = sem("eye_made")
        mask_made = sem("mask_made")
        w0_folded = sem("w0_folded")
        w_hi_made = sem("w_hi_made")
        w_lo_made = sem("w_lo_made")
        b2_scaled = sem("b2_scaled")
        first_ids_loaded = sem("first_ids_loaded")
        ids_loaded = sem("ids_loaded")
        emb_gathered = sem("emb_gathered")
        emb_turned = sem("emb_turned")
        x0_kept = sem("x0_kept")
        x0_stored = sem("x0_stored")
        x0_cols_loaded = sem("x0_cols_loaded")
        dense_loaded = sem("dense_loaded")
        l0_loaded = sem("l0_loaded")
        l0_first_loaded = [sem(f"l0_first_loaded{s}") for s in range(2)]
        left_loaded = [sem(f"left_loaded{s}") for s in range(2)]
        w1s_loaded = sem("w1s_loaded")
        right_loaded = [sem(f"right_loaded{s}") for s in range(2)]
        products_made = sem("products_made")
        hi_made = sem("hi_made")
        lo_made = sem("lo_made")
        products_used = sem("products_used")
        x1_kept = sem("x1_kept")
        x2_kept = sem("x2_kept")
        x1_stored = [sem(f"x1_stored{s}") for s in range(2)]
        x1_summed = sem("x1_summed")
        z1_made = sem("z1_made")
        pair_turned = sem("pair_turned")
        pair_kept = sem("pair_kept")
        g_made = sem("g_made")
        g_kept = sem("g_kept")
        z3_made = sem("z3_made")
        z3_kept = sem("z3_kept")
        last_x2_turned = sem("last_x2_turned")
        last_x0_turned = sem("last_x0_turned")
        last_x2_kept = sem("last_x2_kept")
        last_diag_made = sem("last_diag_made")
        last_g_made = [sem(f"last_g_made{k}") for k in range(2)]
        last_g_kept = [sem(f"last_g_kept{k}") for k in range(2)]
        h1_made = sem("h1_made")
        h1_kept = sem("h1_kept")
        h2_made = sem("h2_made")
        h2_kept = sem("h2_kept")
        y_made = sem("y_made")
        y_kept = sem("y_kept")
        y_stored = sem("y_stored")

        x2_banks = (turn_ps[:, :], x1_ps[:, :])
        x0_banks = (x2_ps[:, 0, :], x2_ps[:, 1, :])
        g_by_sample = g_sb[:, :, :].rearrange("k j (b c) -> k c j b", c=GROUPS)

        x0_cols = shared[0:F, :]
        wt1d_sb = shared[64:64 + D, 0:M1]
        dense_sb = shared[64:64 + D, M1:M1 + BT]
        w0a_sb = x2[0:P0, 0:NT0 * H].rearrange("p (t h) -> p t h", t=NT0)
        w0b_sb = x2[0:P0, NT0 * H:2 * NT0 * H].rearrange("p (t h) -> p t h", t=NT0)
        w1s_sb = l1_right[:, :, :].rearrange("p m n -> p (m n)")[:, 0:2 * NG * SPLIT * H].rearrange("p (t h) -> p t h", h=H)

        block = ctx.enter_context(nc.Block())

        @block.sync
        def _(sp):
            def load_l0_first():
                sp.dma_start(l0_left[:, :], bass.AP(x0_rows, 0, [[0, ND], [COLS, F], [1, N]])).then_inc(l0_first_loaded[0], 16)
                for k0, k1 in ((0, HALF), (HALF, NT0)):
                    for delta in range(ND):
                        rows = slice(F * delta, F * (delta + 1))
                        src = x0_rows[0, ND * k0 + delta, 0:N]
                        sp.dma_start(l0_right[rows, k0:k1, :],
                                     bass.AP(x0_rows, src.offset, [[COLS, F], [ND * COLS, k1 - k0], [1, N]])
                                     ).then_inc(l0_first_loaded[k0 // HALF], 16)

            def load_l0(t, q):
                cols = slice(q * N, (q + 1) * N)
                src = x0_rows[bass.ds(t, 1), 0:1, cols]
                sp.dma_start(l0_left[:, :], bass.AP(x0_rows, src.offset, [[0, ND], [COLS, F], [1, N]])).then_inc(l0_loaded, 16)
                for delta in range(ND):
                    rows = slice(F * delta, F * (delta + 1))
                    src = x0_rows[bass.ds(t, 1), delta:delta + 1, cols]
                    sp.dma_start(l0_right[rows, :, :],
                                 bass.AP(x0_rows, src.offset, [[COLS, F], [ND * COLS, NT0], [1, N]])).then_inc(l0_loaded, 16)

            def load_left(t, q, part):
                for g in range(part * LG[0], part * LG[0] + LG[part]):
                    src = x0_rows[bass.ds(t, 1), JJ * g:JJ * g + 1, q * N:(q + 1) * N]
                    sp.dma_start(l1_left[:, g, :], bass.AP(x0_rows, src.offset, [[COLS, JJ], [0, KK], [1, N]])
                                 ).then_inc(left_loaded[part], 16)

            def store_x1(t, q):
                sp.dma_start(x1_rows[bass.ds(t, 1), q, :, :].rearrange("o h n -> h o n"),
                             x1[:, q % 2, :].unsqueeze(1)).then_inc(x1_stored[q % 2], 16)

            def load_right(t, q, half):
                src = x1_rows[bass.ds(t, 1), q, HALF * KK * half:HALF * KK * half + 1, :]
                sp.dma_start(l1_right[:, HALF * half:HALF * (half + 1), :].rearrange("p m n -> p (m n)"),
                             bass.AP(x1_rows, src.offset, [[0, JJ], [HALF * N, KK], [1, HALF * N]])
                             ).then_inc(right_loaded[half], 16)

            def store_x0(t):
                sp.wait_ge(x0_kept, t + 1)
                wrap = ROWS - F
                full, rest = wrap * D // 128, wrap * D % 128
                for rows, g0, ng, at in ((128, 0, NX - 1, 0), (XLAST, NX - 1, 1, 0),
                                         (128, 0, full, F), (rest, full, 1, F)):
                    dst = x0_rows[bass.ds(t, 1), at:at + 1, 0:BT]
                    sp.dma_start(
                        bass.AP(x0_rows, dst.offset + g0 * 128 * BT, [[BT, rows], [128 * BT, ng], [1, BT]]),
                        x0_turned[0:rows, g0:g0 + ng, :],
                    ).then_inc(x0_stored, 16)

            sp.dma_start(ids_sb[:, :], ids[0:BT, :]).then_inc(first_ids_loaded, 16)
            sp.dma_start(w1s_sb, w1s).then_inc(w1s_loaded, 16)
            for dst, src in ((w0a_sb, w0a), (w0b_sb, w0b), (bias[:, 0:1], b0), (bias[:, 1:2], b1),
                             (bias[:, 2:3], b2), (bias[:, 4:4 + C1], bt1), (bias[:, 4 + C1:4 + C1 + C2], bt2),
                             (w1_sb[:, :, :], w1), (w2_sb[:, :, :], w2), (wt1_sb[:, :, :], wt1),
                             (wt1d_sb, wt1d), (wt2_sb[:, :, :], wt2), (wt3_sb[:, :], wt3)):
                sp.dma_start(dst, src).then_inc(weights_loaded, 16)

            store_x0(0)
            sp.wait_ge(x0_stored, 64)
            load_l0_first()
            for part in range(2):
                load_left(0, 0, part)
            sp.wait_ge(products_made, LEAD)
            load_l0(0, 1)
            sp.wait_ge(x1_kept, 1)
            store_x1(0, 0)
            sp.wait_ge(x1_stored[0], 16)
            sp.wait_ge(w_lo_made, 2)
            for half in range(2):
                load_right(0, 0, half)

            def tile(t, first=False, last=False):
                for q in range(Q):
                    i = q * CI
                    nt, nq = (t, q + 1) if q + 1 < Q else (t + 1, 0)
                    nnt, nnq = (t, q + 2) if q + 2 < Q else (t + 1, q + 2 - Q)
                    if not (last and q + 2 >= Q):
                        sp.wait_ge(products_made, items_made(t, i + L0_ITEMS - 1))
                        load_l0(nnt, nnq)
                    if not (last and q == Q - 1):
                        sp.wait_ge(x1_kept, Q * t + q + 2)
                        store_x1(nt, nq)
                    if q == 0 and not last:
                        store_x0(t + 1)
                    if q == Q - 1:
                        if last:
                            sp.wait_ge(pair_turned, NP * t)
                        sp.dma_start(x0_cols.unsqueeze(1), x0_rows[bass.ds(t, 1), 0:F, :].rearrange("o f n -> f o n")
                                     ).then_inc(x0_cols_loaded, 16)
                    if not (last and q == Q - 1):
                        sp.wait_ge(hi_made, items_made(t, i + L0_ITEMS + NG - 1))
                        load_right(nt, nq, 0)
                        sp.wait_ge(products_made, items_made(t, i + L0_ITEMS + NG + LG[0] - 1))
                        load_left(nt, nq, 0)
                        sp.wait_ge(products_made, items_made(t, i + CI - 1))
                        load_left(nt, nq, 1)
                        load_right(nt, nq, 1)
                    if q == Q - 1:
                        if not first:
                            sp.wait_ge(y_kept, t)
                            sp.dma_start(y_out[:, bass.ds((t - 1) * BT, BT)], y_sb[:, :]).then_inc(y_stored, 16)
                        sp.dma_start(dense_sb, dense_t[:, bass.ds(t * BT, BT)]).then_inc(dense_loaded, 16)

            tile(0, first=True)
            with sp.Fori(1, T - 1) as t:
                tile(t)
            tile(T - 1, last=True)
            sp.wait_ge(y_kept, T)
            sp.dma_start(y_out[:, (T - 1) * BT:], y_sb[:, :]).then_inc(y_stored, 16)
            sp.wait_ge(y_stored, 16 * T)

        @block.gpsimd
        def _(pool):
            nc.gpsimd.memset(eye[:, :], 0.0).then_inc(eye_made, 1)
            pool.wait_ge(eye_made, 1)
            nc.gpsimd.affine_select(out=eye[:, :], in_=eye[:, :], compare_op=ALU.not_equal, fill=1.0, base=0,
                                    pattern=[[-1, 128]], channel_multiplier=1).then_inc(eye_made, 1)

            def gather():
                for f in range(F):
                    pool.indirect_dma_start(
                        out=emb[:, f, :], out_offset=None, in_=tables[f],
                        in_offset=bass.IndirectOffsetOnAxis(ap=ids_sb[:, f:f + 1], axis=0),
                    ).then_inc(emb_gathered, 16)

            pool.wait_ge(first_ids_loaded, 16)
            gather()
            with pool.Fori(16, 16 * (T - 1) + 1, 16) as t16:
                pool.wait_ge(emb_turned, t16 // 16)
                pool.dma_start(ids_sb[:, :], ids[bass.ds(t16 * (BT // 16), BT), :]).then_inc(ids_loaded, 16)
                pool.wait_ge(eye_made, 2)
                pool.wait_ge(ids_loaded, t16)
                gather()

        @block.scalar
        def _(act):
            def keep_x0(t):
                act.wait_ge(emb_turned, t + 1)
                if not isinstance(t, int) or t > 0:
                    act.wait_ge(x0_stored, 64 * t)
                nc.scalar.activation(x0_turned[:, 0:NX - 1, :], g_ps[:, 0, :].rearrange("p (g b) -> p g b", b=BT), ACT.Copy)
                nc.scalar.activation(x0_turned[0:XLAST, NX - 1, :], g_ps[0:XLAST, 1, 0:BT], ACT.Copy).then_inc(x0_kept, 1)

            def keep_x1(t, q, used, early=False):
                act.wait_ge(products_used, used)
                if not early:
                    act.wait_ge(x1_stored[q % 2], 16 * (2 * t + q // 2))
                    act.wait_ge(x1_summed, Q * t + q - 1)
                nc.scalar.activation(x1[:, q % 2, :], x1_ps[:, :], ACT.Identity, bias=bias[:, 0:1]).then_inc(x1_kept, 1)

            def keep_x2(t, q, last=False):
                act.wait_ge(products_used, items_made(t, q * CI + CI - 1, last))
                nc.scalar.activation(x2[:, q * N:(q + 1) * N], x2_ps[:, q % 2, :], ACT.Identity,
                                     bias=bias[:, 1:2]).then_inc(x2_kept, 1)

            def place_diag(p, b):
                return nc.scalar.activation(x0_diag[:, p % 2, :, 0:F, b],
                                            turn_ps[:, 2 * H:2 * H + 2 * F].rearrange("p (i j) -> p i j", i=2),
                                            ACT.Copy, scale=x0_diag[:, 0, 0, F, b:b + 1])

            def tail(n, i):
                if i in TURN:
                    p = TURN.index(i)
                    act.wait_ge(pair_turned, NP * n + p + 1)
                    nc.scalar.activation(x2_turned[:, p % 2, :, :], turn_ps[:, 0:2 * H].rearrange("p (i h) -> p i h", i=2),
                                         ACT.Copy)
                    for b in range(SB // 2):
                        place_diag(p, b)
                if i - 1 in TURN:
                    p = TURN.index(i - 1)
                    for b in range(SB // 2, SB):
                        end = place_diag(p, b)
                    end.then_inc(pair_kept, 1)
                if i in CONTRACT:
                    p = CONTRACT.index(i)
                    act.wait_ge(g_made, NP * n + p + 1)
                    nc.scalar.activation(
                        g_by_sample[:, 2 * p:2 * p + 2, :, :],
                        g_ps[:, :, 0:FS * SB].rearrange("k i (j b) -> k i j b", b=SB), ACT.Copy).then_inc(g_kept, 1)
                if i == L2[-1]:
                    act.wait_ge(z3_made, n + 1)
                    nc.scalar.activation(z3[:, :], mlp_ps[:, 0:BT], ACT.Identity, bias=bias[:, 3:4]).then_inc(z3_kept, 1)
                if i == MLP1[-1]:
                    act.wait_ge(h1_made, n + 1)
                    for m in range(C1):
                        end = nc.scalar.activation(h1[:, m, :], mlp_ps[:, m * BT:(m + 1) * BT], ACT.Relu,
                                                   bias=bias[:, 4 + m:5 + m])
                    end.then_inc(h1_kept, 1)
                if i == MLP2:
                    act.wait_ge(h2_made, n + 1)
                    for m in range(C2):
                        end = nc.scalar.activation(h2[:, m, :], mlp_ps[:, m * BT:(m + 1) * BT], ACT.Relu,
                                                   bias=bias[:, 4 + C1 + m:5 + C1 + m])
                    end.then_inc(h2_kept, 1)
                if i == MLP3:
                    act.wait_ge(y_made, n + 1)
                    nc.scalar.activation(y_sb[:, :], mlp_ps[0:1, 0:BT], ACT.Copy).then_inc(y_kept, 1)
                if i == ITEMS - 1:
                    act.wait_ge(y_stored, 16 * (n + 1))

            def split_item(t, i, last=False):
                n, whole = tiles_of(i)
                rows = P0 if is_l0(i) else 128
                act.wait_ge(products_made, items_made(t, i, last))
                free = slot_free(t, i, 2, last)
                if free is not None:
                    act.wait_ge(products_used, free)
                nc.scalar.activation(products_hi[0:rows, i % 2, :, :], products[0:rows, i % RING, whole:n, :],
                                     ACT.Copy).then_inc(hi_made, 1)

            act.wait_ge(b2_scaled, 1)
            act.wait_ge(mask_made, 4)
            act.wait_ge(w0_folded, 3)
            nc.scalar.activation(w0_hi[:, 0:SPLIT, :], w0a_sb[:, HALF - SPLIT:HALF, :], ACT.Copy)
            nc.scalar.activation(w0_hi[:, SPLIT:, :], w0a_sb[:, NT0 - SPLIT:, :], ACT.Copy).then_inc(w_hi_made, 1)
            act.wait_ge(w1s_loaded, 16)
            nc.scalar.activation(w1_hi[:, :, :], w1s_sb, ACT.Copy).then_inc(w_hi_made, 1)
            keep_x0(0)
            for i in FIRST:
                split_item(0, i)
            keep_x1(0, 0, LEAD, early=True)
            for i in (0, 1):
                split_item(0, i)

            def tile(t, first=False, last=False):
                for i in range(ITEMS):
                    q = i // CI
                    if i % CI == L0_ITEMS + NG - 3 and not (last and q == Q - 1):
                        nt, nq = (t, q + 1) if q + 1 < Q else (t + 1, 0)
                        act.wait_ge(x1_stored[nq % 2], 16 * (2 * nt + nq // 2 + 1))
                    if i + 2 >= ITEMS:
                        if not last:
                            split_item(t + 1, i + 2 - ITEMS)
                    elif not skipped(i + 2, last):
                        split_item(t, i + 2, last)
                    if i % CI == L0_ITEMS - 1 and not skipped(i, last):
                        if q + 1 < Q:
                            if q == 1 and not last:
                                act.wait_ge(x0_stored, 64 * (t + 2))
                            keep_x1(t, q + 1, items_made(t, i, last), early=first and q == 0)
                        else:
                            keep_x1(t + 1, 0, items_made(t, i, last))
                    if i == (FIRST_TURN_EMB if first else TURN_EMB) and not last:
                        keep_x0(t + 1)
                    if not first:
                        tail(t - 1, i)
                    if i == KEEP_X2:
                        keep_x2(t, 0, last)
                    if i % CI == CI - 1 and q > 0:
                        keep_x2(t, q, last)

            tile(0, first=True)
            with act.Fori(1, T - 1) as t:
                tile(t)
            tile(T - 1, last=True)
            def keep_last_g(p):
                act.wait_ge(last_g_made[0], p + 1)
                nc.scalar.activation(g_by_sample[:, 2 * p, :, :], g_ps[:, 0, 0:FS * SB].rearrange("k (j b) -> k j b", b=SB),
                                     ACT.Copy).then_inc(last_g_kept[0], 1)

            for p in range(NP):
                act.wait_ge(last_x2_turned, p + 1)
                if p >= 2:
                    act.wait_ge(last_g_made[1], p - 1)
                nc.scalar.activation(x2_turned[:, p % 2, :, :], x2_banks[p % 2][:, 0:2 * H].rearrange("p (i h) -> p i h", i=2),
                                     ACT.Copy).then_inc(last_x2_kept, 1)
                if p > 0:
                    keep_last_g(p - 1)
            keep_last_g(NP - 1)
            for i in range(L2[0], MLP3 + 1):
                tail(T - 1, i)

        @block.vector
        def _(dve):
            dve.wait_ge(weights_loaded, 16 * 13)
            dve.wait_ge(w1s_loaded, 16)
            whole = HALF - SPLIT
            nc.vector.tensor_tensor(w0_sb[:, 0:whole, :], w0a_sb[:, 0:whole, :], w0b_sb[:, 0:whole, :], ALU.add).then_inc(w0_folded, 1)
            nc.vector.tensor_tensor(w0_sb[:, whole:, :], w0a_sb[:, HALF:NT0 - SPLIT, :], w0b_sb[:, HALF:NT0 - SPLIT, :],
                                    ALU.add).then_inc(w0_folded, 1)
            dve.wait_ge(w0_folded, 2)
            nc.vector.tensor_tensor(w0a_sb, w0a_sb, w0b_sb, ALU.add).then_inc(w0_folded, 1)
            nc.vector.tensor_scalar(bias[:, 3:4], bias[:, 2:3], float(D), None, ALU.mult).then_inc(b2_scaled, 1)
            dve.wait_ge(eye_made, 2)
            nc.vector.tensor_reduce(x0_diag[:, 0, 0, F, :], eye[:, :].rearrange("p (d b) -> p b d", b=SB),
                                    AX.X, ALU.add).then_inc(mask_made, 1)
            dve.wait_ge(mask_made, 1)
            for s, i in ((0, 1), (1, 0), (1, 1)):
                nc.vector.tensor_copy(x0_diag[:, s, i, F, :], x0_diag[:, 0, 0, F, :]).then_inc(mask_made, 1)
            dve.wait_ge(mask_made, 4)

            dve.wait_ge(w_hi_made, 1)
            nc.vector.tensor_tensor(w0_lo[:, 0:SPLIT, :], w0a_sb[:, HALF - SPLIT:HALF, :], w0_hi[:, 0:SPLIT, :].bitcast(fp32), ALU.subtract)
            nc.vector.tensor_tensor(w0_lo[:, SPLIT:, :], w0a_sb[:, NT0 - SPLIT:, :], w0_hi[:, SPLIT:, :].bitcast(fp32),
                                    ALU.subtract).then_inc(w_lo_made, 1)
            dve.wait_ge(w_hi_made, 2)
            nc.vector.tensor_tensor(w1_lo[:, :, :], w1s_sb, w1_hi[:, :, :].bitcast(fp32), ALU.subtract).then_inc(w_lo_made, 1)

            def multiply(t, i):
                q, n = i // CI, tiles_of(i)[0]
                slot = i % RING
                if is_l0(i):
                    at = HALF * (i % CI)
                    if i in FIRST:
                        dve.wait_ge(l0_first_loaded[FIRST.index(i)], 16 * (1 + ND if i == FIRST[0] else ND))
                    elif i % CI == 0:
                        dve.wait_ge(l0_loaded, 16 * (1 + ND) * (Q * t + q + 1))
                    left, right = l0_left[:, :], l0_right[:, at:at + n, :]
                    out = products[0:P0, slot, 0:n, :]
                else:
                    half, g = l1_item(i)
                    c = Q * t + q + 1
                    if half == 0 and g == 0:
                        dve.wait_ge(left_loaded[0], 16 * LG[0] * c)
                    if half == 0 and g == LG[0]:
                        dve.wait_ge(left_loaded[1], 16 * LG[1] * c)
                    if g == 0:
                        dve.wait_ge(right_loaded[half], 16 * c)
                    left, right = l1_left[:, g, :], l1_right[:, HALF * half:HALF * (half + 1), :]
                    out = products[:, slot, :, :]
                nc.vector.tensor_tensor(out, left.unsqueeze(1).broadcast_to([left.shape[0], n, N]), right,
                                        ALU.mult).then_inc(products_made, 1)

            def split_item(t, i, last=False):
                n, whole = tiles_of(i)
                rows = P0 if is_l0(i) else 128
                dve.wait_ge(hi_made, items_made(t, i, last))
                nc.vector.tensor_tensor(products_lo[0:rows, i % 2, :, :], products[0:rows, i % RING, whole:n, :],
                                        products_hi[0:rows, i % 2, :, :].bitcast(fp32), ALU.subtract).then_inc(lo_made, 1)

            def sum_x1(t, q):
                dve.wait_ge(x1_kept, Q * t + q + 1)
                if q == 0 and not (isinstance(t, int) and t == 0):
                    dve.wait_ge(z1_made, t)
                nc.vector.tensor_reduce(z1_parts[:, q, :], x1[:, q % 2, :].rearrange("h (d b) -> h b d", b=BT),
                                        AX.X, ALU.add).then_inc(x1_summed, 1)

            def sum_z1(t):
                dve.wait_ge(x1_summed, Q * t + Q)
                if not isinstance(t, int) or t > 0:
                    dve.wait_ge(h1_made, t)
                nc.vector.tensor_reduce(z1[:, :], z1_parts[:, :, :].rearrange("h q b -> h b q"),
                                        AX.X, ALU.add).then_inc(z1_made, 1)

            for i in FIRST:
                multiply(0, i)
            for i in FIRST:
                split_item(0, i)

            def tile(t, first=False, last=False):
                for i in range(ITEMS):
                    q, r = i // CI, i % CI
                    if not skipped(i, last):
                        free = slot_free(t, i, RING, last)
                        if free is not None:
                            dve.wait_ge(products_used, free)
                        multiply(t, i)
                        if not skipped(i - 1, last) and not (first and i == 0):
                            split_item(t, i - 1, last)
                    elif i % CI == 0:
                        split_item(t, i - 1)
                    if first and i == 1:
                        sum_x1(0, 0)
                    if q + 1 < Q and r == L0_ITEMS + RING:
                        sum_x1(t, q + 1)
                    if i == SUM_Z1:
                        sum_z1(t)
                    if i == SUM_Z1 + 1 and not last:
                        sum_x1(t + 1, 0)

            tile(0, first=True)
            with dve.Fori(1, T - 1) as t:
                tile(t)
            tile(T - 1, last=True)
            split_item(T - 1, ITEMS - 1, last=True)

            def keep_last_g(p):
                dve.wait_ge(last_g_made[1], p + 1)
                nc.vector.tensor_copy(g_by_sample[:, 2 * p + 1, :, :], g_ps[:, 1, 0:FS * SB].rearrange("k (j b) -> k j b", b=SB)
                                      ).then_inc(last_g_kept[1], 1)

            for p in range(NP):
                dve.wait_ge(last_x0_turned, p + 1)
                if p >= 2:
                    dve.wait_ge(last_g_made[1], p - 1)
                for k in range(2):
                    end = nc.vector.tensor_tensor(
                        x0_diag[:, p % 2, k, 0:F, :],
                        x0_banks[p % 2][:, k * F:(k + 1) * F].unsqueeze(2).broadcast_to([128, F, SB]),
                        x0_diag[:, p % 2, k, F, :].unsqueeze(1).broadcast_to([128, F, SB]), ALU.mult)
                end.then_inc(last_diag_made, 1)
                if p > 0:
                    keep_last_g(p - 1)
            keep_last_g(NP - 1)

        @block.tensor
        def _(pe):
            mm = nc.tensor.matmul

            def turn_emb(t):
                pe.wait_ge(emb_gathered, 16 * F * (t + 1))
                flat = emb[:, :, :].rearrange("b f d -> b (f d)")
                for g in range(NX):
                    rows = XLAST if g == NX - 1 else 128
                    last = nc.tensor.transpose(g_ps[0:rows, g // 4, (g % 4) * BT:(g % 4 + 1) * BT],
                                               flat[:, 128 * g:128 * g + rows], eye[:, :])
                last.then_inc(emb_turned, 1)

            def contract(out, w, w_hi, w_lo, at, at_split, rows, i, made, first, last):
                n, whole = tiles_of(i)
                for k in range(whole):
                    mm(out, w[:, at + k, :], products[0:rows, i % RING, k, :], start=first and k == 0, stop=False)
                pe.wait_ge(lo_made, made)
                for k in range(SPLIT):
                    hi = products_hi[0:rows, i % 2, k, :]
                    mm(out, w_hi[:, at_split + k, :], hi, start=False, stop=False)
                    mm(out, w_hi[:, at_split + k, :], products_lo[0:rows, i % 2, k, :], start=False, stop=False)
                    end = mm(out, w_lo[:, at_split + k, :], hi, start=False, stop=last and k == SPLIT - 1)
                end.then_inc(products_used, 1)

            def layer0(t, i, made):
                c = Q * t + i // CI + 1
                half = i % CI
                pe.wait_ge(products_made, made)
                if half == 0 and not (isinstance(c, int) and c < 1):
                    pe.wait_ge(x1_kept, c)
                contract(x1_ps[:, :], w0_sb, w0_hi, w0_lo, (HALF - SPLIT) * half, SPLIT * half, P0, i, made,
                         half == 0, half == 1)

            def layer1(t, i, made):
                q = i // CI
                c = Q * t + q
                half, g = l1_item(i)
                pe.wait_ge(products_made, made)
                if g == 0 and half == 0 and not (isinstance(c, int) and c < 2):
                    pe.wait_ge(x2_kept, c - 1)
                at = NG * half + g
                contract(x2_ps[:, q % 2, :], w1_sb, w1_hi, w1_lo, (HALF - SPLIT) * at, SPLIT * at, 128, i, made,
                         at == 0, at == 2 * NG - 1)

            def tail(n, i, last=False):
                if i in TURN:
                    p = TURN.index(i)
                    if p == 0:
                        pe.wait_ge(x2_kept, Q * (n + 1))
                        pe.wait_ge(x0_cols_loaded, 16 * (n + 1))
                    for k in range(2):
                        nc.tensor.transpose(turn_ps[:, k * H:(k + 1) * H], x2[:, 2 * p + k::GROUPS], eye[:, :])
                    for k in range(2):
                        end = nc.tensor.transpose(turn_ps[:, 2 * H + k * F:2 * H + (k + 1) * F],
                                                  x0_cols[:, 2 * p + k::GROUPS], eye[0:F, 0:F])
                    end.then_inc(pair_turned, 1)
                if i in CONTRACT:
                    p = CONTRACT.index(i)
                    pe.wait_ge(pair_kept, NP * n + p + 1)
                    if p > 0:
                        pe.wait_ge(g_kept, NP * n + p)
                    for k in range(2):
                        end = mm(g_ps[:, k, 0:FS * SB], x2_turned[:, p % 2, k, :],
                                 x0_diag[:, p % 2, k, :, :].rearrange("p j b -> p (j b)"), start=True, stop=True)
                    end.then_inc(g_made, 1)
                if i in L2:
                    part = L2.index(i)
                    if part == 0 and not last:
                        pe.wait_ge(g_kept, NP * (n + 1))
                    for j in range(F * part // len(L2), F * (part + 1) // len(L2)):
                        end = mm(mlp_ps[:, 0:BT], w2_sb[:, j, :], g_sb[:, j, :], start=j == 0, stop=j == F - 1)
                    if part == len(L2) - 1:
                        end.then_inc(z3_made, 1)
                if i in MLP1:
                    part = MLP1.index(i)
                    if part == 0:
                        pe.wait_ge(z3_kept, n + 1)
                        pe.wait_ge(z1_made, n + 1)
                        pe.wait_ge(dense_loaded, 16 * (n + 1))
                    for m in range(C1 * part // 2, C1 * (part + 1) // 2):
                        out = mlp_ps[:, m * BT:(m + 1) * BT]
                        cols = slice(128 * m, 128 * (m + 1))
                        for k, z in enumerate((z1[:, :], g_sb[:, F, :], z3[:, :])):
                            mm(out, wt1_sb[:, k, cols], z, start=k == 0, stop=False)
                        end = mm(out, wt1d_sb[:, cols], dense_sb, start=False, stop=True)
                    if part == 1:
                        end.then_inc(h1_made, 1)
                if i == MLP2:
                    pe.wait_ge(h1_kept, n + 1)
                    for m in range(C2):
                        for k in range(C1):
                            end = mm(mlp_ps[:, m * BT:(m + 1) * BT], wt2_sb[:, k, 128 * m:128 * (m + 1)], h1[:, k, :],
                                     start=k == 0, stop=k == C1 - 1)
                    end.then_inc(h2_made, 1)
                if i == MLP3:
                    pe.wait_ge(h2_kept, n + 1)
                    for k in range(C2):
                        end = mm(mlp_ps[0:1, 0:BT], wt3_sb[:, k:k + 1], h2[:, k, :], start=k == 0, stop=k == C2 - 1)
                    end.then_inc(y_made, 1)
                if i == END:
                    pe.wait_ge(y_kept, n + 1)

            pe.wait_ge(eye_made, 2)
            turn_emb(0)
            pe.wait_ge(w_lo_made, 2)
            pe.wait_ge(x0_stored, 64)
            for _ in range(WARM):
                mm(x2_ps[:, 0, :], w2_sb[:, 0, :], w2_sb[:, 0:4, :].rearrange("p j h -> p (j h)"), start=True, stop=True)
            for i in FIRST:
                layer0(0, i, items_made(0, i))

            def tile(t, first=False, last=False):
                for i in range(ITEMS):
                    if not skipped(i, last):
                        (layer0 if is_l0(i) else layer1)(t, i, items_made(t, i, last))
                    if i == (FIRST_TURN_EMB if first else TURN_EMB) and not last:
                        turn_emb(t + 1)
                    if i == CONTRACT[0] and not (first or last):
                        pe.wait_ge(x0_kept, t + 2)
                    if not first:
                        tail(t - 1, i)

            tile(0, first=True)
            with pe.Fori(1, T - 1) as t:
                tile(t)
            tile(T - 1, last=True)

            def contract_last(p):
                pe.wait_ge(last_x2_kept, p + 1)
                pe.wait_ge(last_diag_made, p + 1)
                for k in range(2):
                    if p > 0:
                        pe.wait_ge(last_g_kept[k], p)
                    mm(g_ps[:, k, 0:FS * SB], x2_turned[:, p % 2, k, :],
                       x0_diag[:, p % 2, k, :, :].rearrange("p j b -> p (j b)"), start=True, stop=True).then_inc(last_g_made[k], 1)

            for p in range(NP):
                if p == 0:
                    pe.wait_ge(x0_cols_loaded, 16 * T)
                if p >= 2:
                    pe.wait_ge(last_diag_made, p - 1)
                for k in range(2):
                    end = nc.tensor.transpose(x0_banks[p % 2][:, k * F:(k + 1) * F], x0_cols[:, 2 * p + k::GROUPS], eye[0:F, 0:F])
                end.then_inc(last_x0_turned, 1)
                if p == 0:
                    pe.wait_ge(x2_kept, Q * T)
                if p >= 2:
                    pe.wait_ge(last_x2_kept, p - 1)
                for k in range(2):
                    end = nc.tensor.transpose(x2_banks[p % 2][:, k * H:(k + 1) * H], x2[:, 2 * p + k::GROUPS], eye[:, :])
                end.then_inc(last_x2_turned, 1)
                if p > 0:
                    contract_last(p - 1)
            contract_last(NP - 1)
            for k in range(2):
                pe.wait_ge(last_g_kept[k], NP)
            for i in range(L2[0], MLP3 + 1):
                tail(T - 1, i, last=True)


def kernel(**inputs):
    import numpy as np
    import concourse.bacc as bacc
    from concourse.bass_utils import run_bass_kernel_spmd

    W0 = np.asarray(inputs["L0_rec_W0"]).reshape(H, F, F)
    W1 = np.asarray(inputs["L0_rec_W1"]).reshape(H, F, H)
    W2 = np.asarray(inputs["L0_rec_W2"]).reshape(H, F, H)
    Wt1 = np.asarray(inputs["W_top1"])
    Wt2 = np.asarray(inputs["W_top2"])

    j = np.arange(F)[None, :, None]
    delta = np.arange(NT0)[None, None, :] * ND + np.arange(ND)[:, None, None]
    k = (j + delta) % F
    j = np.broadcast_to(j, k.shape)
    w0a = np.zeros((ND, F, NT0, H), W0.dtype)
    w0b = np.zeros((ND, F, NT0, H), W0.dtype)
    once = np.broadcast_to(delta <= F // 2, k.shape)
    both = once & np.broadcast_to(delta > 0, k.shape)
    w0a[once] = W0[:, j[once], k[once]].T
    w0b[both] = W0[:, k[both], j[both]].T

    w1 = np.zeros((H, NG * JJ, H), W1.dtype)
    w1[:, :F] = W1
    w1 = w1.reshape(H, NG, JJ, 2, KK, HALF).transpose(2, 4, 3, 1, 5, 0)
    whole = HALF - SPLIT

    arrays = {
        "ids": np.asarray(inputs["ids"]),
        "dense_t": np.asarray(inputs["dense_ctx"]).T,
        "w0a": w0a.reshape(P0, NT0, H),
        "w0b": w0b.reshape(P0, NT0, H),
        "b0": np.asarray(inputs["L0_rec_b0"]).reshape(H, 1),
        "w1": w1[..., :whole, :].reshape(128, -1, H),
        "w1s": w1[..., whole:, :].reshape(128, -1, H),
        "b1": np.asarray(inputs["L0_rec_b1"]).reshape(H, 1),
        "w2": W2.transpose(2, 1, 0),
        "b2": np.asarray(inputs["L0_rec_b2"]).reshape(H, 1),
        "wt1": Wt1[:3 * H].reshape(3, H, M1).transpose(1, 0, 2),
        "wt1d": Wt1[3 * H:],
        "bt1": np.asarray(inputs["b_top1"]).reshape(C1, 128).T,
        "wt2": Wt2.reshape(C1, 128, M2).transpose(1, 0, 2),
        "bt2": np.asarray(inputs["b_top2"]).reshape(C2, 128).T,
        "wt3": np.asarray(inputs["W_top3"]).reshape(C2, 128).T,
    }
    for f in range(F):
        arrays[f"tbl_{f}"] = np.asarray(inputs[f"tbl_{f}"])

    nc = bacc.Bacc("TRN2", target_bir_lowering=False, num_devices=1)
    aps = {}
    for name in arrays:
        arrays[name] = np.ascontiguousarray(arrays[name])
        aps[name] = nc.dram_tensor(f"in_{name}", arrays[name].shape, mybir.dt.from_np(arrays[name].dtype),
                                   kind="ExternalInput").ap()
    y_out = nc.dram_tensor("out_y", (1, B), mybir.dt.float32, kind="ExternalOutput").ap()
    build(nc, aps["ids"], [aps[f"tbl_{f}"] for f in range(F)], *[aps[n] for n in (
        "dense_t", "w0a", "w0b", "b0", "w1", "w1s", "b1", "w2", "b2", "wt1", "wt1d", "bt1", "wt2", "bt2", "wt3")], y_out)
    r = run_bass_kernel_spmd(nc, [{f"in_{name}": a for name, a in arrays.items()}], core_ids=[0])
    return r.results[0]["out_y"].reshape(B, 1)
```

```python
import concourse.bass as bass
from concourse import mybir
from contextlib import ExitStack

B, F, D, H = 1024, 39, 16, 128
BT = 128
T = B // BT
COLS = BT * D
N = 512
Q = COLS // N
JJ, KK = 8, 16
NG = F // JJ
NW = F - NG * JJ
NM = H // KK
ND = 3
NT0 = (F // 2 + 1 + ND - 1) // ND
P0 = ND * F
ROWS = F + ND * NT0 - 1
HALF = 4
RING = 3
SPLIT = 2
L0_ITEMS = 2
WIDE = (L0_ITEMS, L0_ITEMS + NG + 1)
CI = WIDE[1] + NG + 1
ITEMS = Q * CI
LG = (2, 2)
LEAD = L0_ITEMS
FIRST = (-CI, -CI + 1)
FS = F + 1
SB = BT // D
GROUPS = BT // SB
NP = GROUPS // 2
NX = (F * D + 127) // 128
XLAST = F * D - 128 * (NX - 1)
HOT = (2, 3, 4, 7, 8, 9, 11, 12)
VP, VB = 125, 8
HOT_RUNS = ((2, 5), (7, 10), (11, 13))
HOT_RING = 5
EVERY = 3
TURN = [1 + EVERY * p for p in range(NP)]
CONTRACT = [m + 2 for m in TURN]
Z1_IN = CONTRACT[-1] + 1
L2 = [Z1_IN + 1 + n for n in range(11)]
MLP1 = [L2[-1] + 2 + n for n in range(4)]
MLP2 = [MLP1[-1] + 2, MLP1[-1] + 3]
MLP3 = MLP2[-1] + 2
SUM_Z1 = MLP1[-1]
TURN_EMB, FIRST_TURN_EMB = TURN[0], 6
WARM = 6
KEEP_X2 = TURN[-1] + 1
M1, M2 = 512, 256
C1, C2 = M1 // 128, M2 // 128


def items_made(t, i, last=False):
    if isinstance(t, int) and t == 0 and i < 0:
        return i - FIRST[0] + 1
    gone = L0_ITEMS if last and i >= ITEMS - CI + L0_ITEMS else 0
    return LEAD + ITEMS * t + i + 1 - gone


def is_l0(i):
    return i % CI < L0_ITEMS


def skipped(i, last):
    return last and i >= ITEMS - CI and is_l0(i)


def slot_free(t, i, slots, last=False):
    if isinstance(t, int) and t == 0 and i < slots:
        return i + 1 if 0 <= i < LEAD else None
    back = i - slots
    while skipped(back, last):
        back -= slots
    return items_made(t, back, last)


def tiles_of(i):
    n = {1: NT0 - HALF, WIDE[1]: NW - HALF}.get(i % CI, HALF)
    return n, n - SPLIT


W1_WHOLE = sum(tiles_of(i)[1] for i in range(L0_ITEMS, CI))
W1_SPLIT = SPLIT * (CI - L0_ITEMS)


def l1_item(i):
    half, g = divmod(i % CI - L0_ITEMS, NG + 1)
    return half, g - 1


def build(nc, ids, ids_hot, table_rows, tables, dense_t, w0a, w0b, b0, w1, w1s, b1, w2, b2, wt1, wt1d, bt1, wt2, bt2, wt3, y_out):
    fp32 = mybir.dt.float32
    fp32r = mybir.dt.float32r
    i32 = mybir.dt.int32
    ALU = mybir.AluOpType
    ACT = mybir.ActivationFunctionType
    AX = mybir.AxisListType

    x0_rows = nc.dram_tensor("x0_rows", [T, ROWS, COLS], fp32)
    x1_rows = nc.dram_tensor("x1_rows", [T, Q, H, N], fp32)

    ctx = ExitStack()
    with ctx:
        def sb(name, shape, dt=fp32):
            return ctx.enter_context(nc.sbuf_tensor(name, shape, dt))

        def pb(name, shape):
            return ctx.enter_context(nc.psum_tensor(name, shape, fp32))

        def sem(name):
            return ctx.enter_context(nc.semaphore(name))

        w0_sb = sb("w0_sb", [P0, NT0 - 2 * SPLIT, H])
        w0_hi = sb("w0_hi", [P0, 2 * SPLIT, H], fp32r)
        w0_lo = sb("w0_lo", [P0, 2 * SPLIT, H], fp32r)
        w1_sb = sb("w1_sb", [128, W1_WHOLE, H])
        w1_hi = sb("w1_hi", [128, W1_SPLIT, H], fp32r)
        w1_lo = sb("w1_lo", [128, W1_SPLIT, H], fp32r)
        w2_sb = sb("w2_sb", [H, F, H])
        wt1_sb = sb("wt1_sb", [H, 3, M1])
        wt2_sb = sb("wt2_sb", [128, C1, M2])
        wt3_sb = sb("wt3_sb", [128, C2])
        bias = sb("bias", [128, 4 + C1 + C2])
        eye = sb("eye", [128, 128])
        ids_sb = sb("ids_sb", [BT, F], i32)
        emb = sb("emb", [BT, F, D])
        turned_or_hidden = sb("turned_or_hidden", [128, C1 + C2, BT])
        x0_turned = turned_or_hidden[:, 0:NX, :]
        h1 = turned_or_hidden[:, 0:C1, :]
        h2 = turned_or_hidden[:, C1:, :]
        shared = sb("shared", [128, COLS])
        x2 = sb("x2", [H, COLS])
        g_sb = sb("g_sb", [H, FS, BT])
        z1_parts = sb("z1_parts", [H, Q, BT])
        z1 = sb("z1", [H, BT])
        z3 = sb("z3", [H, BT])
        y_sb = sb("y_sb", [1, BT])
        l0_left = sb("l0_left", [P0, N])
        l0_right = sb("l0_right", [P0, NT0, N])
        l1_left = sb("l1_left", [128, NG, N])
        wide_left = sb("wide_left", [128, HALF, N])
        l1_right = sb("l1_right", [128, NM, N])
        x1 = sb("x1", [H, 2, N])
        products = sb("products", [128, RING, HALF, N])
        products_hi = sb("products_hi", [128, 2, SPLIT, N], fp32r)
        products_lo = sb("products_lo", [128, 2, SPLIT, N], fp32r)
        x2_turned = sb("x2_turned", [128, 2, H])
        x0_diag = sb("x0_diag", [128, 2, FS, SB])

        x1_ps = pb("x1_ps", [H, N])
        x2_ps = pb("x2_ps", [H, 2, N])
        turn_ps = pb("turn_ps", [128, N])
        g_ps = pb("g_ps", [128, 2, N])
        z3_ps = pb("z3_ps", [128, N])
        mlp_ps = pb("mlp_ps", [128, N])

        weights_loaded = sem("weights_loaded")
        eye_made = sem("eye_made")
        mask_made = sem("mask_made")
        w0_folded = sem("w0_folded")
        w_hi_made = sem("w_hi_made")
        w_lo_made = sem("w_lo_made")
        b2_scaled = sem("b2_scaled")
        first_ids_loaded = sem("first_ids_loaded")
        ids_loaded = sem("ids_loaded")
        hot_ids_loaded = sem("hot_ids_loaded")
        hot_tables_loaded = sem("hot_tables_loaded")
        one_hot_made = sem("one_hot_made")
        one_hot_used = sem("one_hot_used")
        hot_kept = sem("hot_kept")
        emb_gathered = sem("emb_gathered")
        emb_turned = sem("emb_turned")
        x0_kept = sem("x0_kept")
        x0_stored = sem("x0_stored")
        x0_cols_loaded = sem("x0_cols_loaded")
        dense_loaded = sem("dense_loaded")
        l0_loaded = sem("l0_loaded")
        l0_first_loaded = [sem(f"l0_first_loaded{s}") for s in range(2)]
        left_loaded = [sem(f"left_loaded{s}") for s in range(2)]
        wide_loaded = [sem(f"wide_loaded{s}") for s in range(2)]
        w1s_loaded = sem("w1s_loaded")
        right_loaded = [sem(f"right_loaded{s}") for s in range(2)]
        products_made = sem("products_made")
        hi_made = sem("hi_made")
        lo_made = sem("lo_made")
        products_used = sem("products_used")
        x1_kept = sem("x1_kept")
        x2_kept = sem("x2_kept")
        x1_stored = [sem(f"x1_stored{s}") for s in range(2)]
        x1_summed = sem("x1_summed")
        z1_made = sem("z1_made")
        pair_turned = sem("pair_turned")
        pair_kept = sem("pair_kept")
        g_made = sem("g_made")
        g_kept = sem("g_kept")
        z1_read = sem("z1_read")
        z3_made = sem("z3_made")
        z3_kept = sem("z3_kept")
        last_x2_turned = sem("last_x2_turned")
        last_x0_turned = sem("last_x0_turned")
        last_mask_made = sem("last_mask_made")
        last_x2_kept = sem("last_x2_kept")
        last_diag_made = sem("last_diag_made")
        last_g_made = [sem(f"last_g_made{k}") for k in range(2)]
        last_g_kept = [sem(f"last_g_kept{k}") for k in range(2)]
        h1_made = sem("h1_made")
        h1_kept = sem("h1_kept")
        h2_made = sem("h2_made")
        h2_kept = sem("h2_kept")
        y_made = sem("y_made")
        y_kept = sem("y_kept")
        y_stored = sem("y_stored")

        x2_banks = (turn_ps[:, :], x1_ps[:, :])
        done = products[:, 0, :, :].rearrange("p k n -> p (k n)")
        last_diags = (x0_diag[:, :, :, :], done[:, 0:2 * FS * SB].rearrange("p (i j b) -> p i j b", i=2, j=FS))
        last_x2s = (x2_turned[:, :, :], done[:, 2 * N:2 * N + 2 * H].rearrange("p (i h) -> p i h", i=2))
        x0_banks = (x2_ps[:, 0, :], x2_ps[:, 1, :])
        g_by_sample = g_sb[:, :, :].rearrange("k j (b c) -> k c j b", c=GROUPS)

        l0_left_early = x1[0:P0, 1, :]
        l0_right_early = l1_right[0:P0, 0:NT0, :]

        x0_cols = shared[0:F, :]
        wt1d_sb = shared[64:64 + D, 0:M1]
        dense_sb = shared[64:64 + D, M1:M1 + BT]
        w0a_sb = x2[0:P0, 0:NT0 * H].rearrange("p (t h) -> p t h", t=NT0)
        w0b_sb = x2[0:P0, NT0 * H:2 * NT0 * H].rearrange("p (t h) -> p t h", t=NT0)
        w1s_sb = l1_right[:, :, :].rearrange("p m n -> p (m n)")[:, 0:W1_SPLIT * H].rearrange("p (t h) -> p t h", h=H)

        hot_tables = l1_left[:, :, :].rearrange("p g n -> p (g n)")[0:VP, 0:len(HOT) * VB * D].rearrange(
            "p (f k d) -> p f k d", k=VB, d=D)
        wide_flat = wide_left[:, :, :].rearrange("p k n -> p (k n)")
        hot_ids = wide_flat[0:VP, 0:len(HOT) * BT].bitcast(i32)
        hot_rows = wide_flat[0:VP, len(HOT) * BT:len(HOT) * BT + VB].bitcast(i32)
        one_hot = g_sb[0:VP, 0:HOT_RING * VB, :].rearrange("p (s k) b -> p s k b", k=VB)
        hot_ps = turn_ps[:, 0:len(HOT) * D].rearrange("b (f d) -> b f d", d=D)

        block = ctx.enter_context(nc.Block())

        @block.sync
        def _(sp):
            def load_l0_first():
                sp.dma_start(l0_left[:, :], bass.AP(x0_rows, 0, [[0, ND], [COLS, F], [1, N]])).then_inc(l0_first_loaded[0], 16)
                for k0, k1 in ((0, HALF), (HALF, NT0)):
                    for delta in range(ND):
                        rows = slice(F * delta, F * (delta + 1))
                        src = x0_rows[0, ND * k0 + delta, 0:N]
                        sp.dma_start(l0_right[rows, k0:k1, :],
                                     bass.AP(x0_rows, src.offset, [[COLS, F], [ND * COLS, k1 - k0], [1, N]])
                                     ).then_inc(l0_first_loaded[k0 // HALF], 16)

            def load_l0(t, q, left=l0_left, right=l0_right[:, :, :]):
                cols = slice(q * N, (q + 1) * N)
                src = x0_rows[bass.ds(t, 1), 0:1, cols]
                sp.dma_start(left[0:P0, :], bass.AP(x0_rows, src.offset, [[0, ND], [COLS, F], [1, N]])).then_inc(l0_loaded, 16)
                for delta in range(ND):
                    rows = slice(F * delta, F * (delta + 1))
                    src = x0_rows[bass.ds(t, 1), delta:delta + 1, cols]
                    sp.dma_start(right[rows, :, :],
                                 bass.AP(x0_rows, src.offset, [[COLS, F], [ND * COLS, NT0], [1, N]])).then_inc(l0_loaded, 16)

            def load_left(t, q, part):
                for g in range(part * LG[0], part * LG[0] + LG[part]):
                    src = x0_rows[bass.ds(t, 1), JJ * g:JJ * g + 1, q * N:(q + 1) * N]
                    sp.dma_start(l1_left[:, g, :], bass.AP(x0_rows, src.offset, [[COLS, JJ], [0, KK], [1, N]])
                                 ).then_inc(left_loaded[part], 16)

            def load_wide(t, q, part):
                j = NG * JJ + part * HALF
                n = tiles_of(WIDE[part])[0]
                src = x0_rows[bass.ds(t, 1), j:j + 1, q * N:(q + 1) * N]
                sp.dma_start(wide_left[:, 0:n, :], bass.AP(x0_rows, src.offset, [[0, 128], [COLS, n], [1, N]])
                             ).then_inc(wide_loaded[part], 16)

            def store_x1(t, q):
                sp.dma_start(x1_rows[bass.ds(t, 1), q, :, :].rearrange("o h n -> h o n"),
                             x1[:, q % 2, :].unsqueeze(1)).then_inc(x1_stored[q % 2], 16)

            def load_right(t, q, half):
                src = x1_rows[bass.ds(t, 1), q, HALF * KK * half:HALF * KK * half + 1, :]
                sp.dma_start(l1_right[:, HALF * half:HALF * (half + 1), :].rearrange("p m n -> p (m n)"),
                             bass.AP(x1_rows, src.offset, [[0, JJ], [HALF * N, KK], [1, HALF * N]])
                             ).then_inc(right_loaded[half], 16)

            def store_x0(t):
                sp.wait_ge(x0_kept, t + 1)
                wrap = ROWS - F
                full, rest = wrap * D // 128, wrap * D % 128
                for rows, g0, ng, at in ((128, 0, NX - 1, 0), (XLAST, NX - 1, 1, 0),
                                         (128, 0, full, F), (rest, full, 1, F)):
                    dst = x0_rows[bass.ds(t, 1), at:at + 1, 0:BT]
                    sp.dma_start(
                        bass.AP(x0_rows, dst.offset + g0 * 128 * BT, [[BT, rows], [128 * BT, ng], [1, BT]]),
                        x0_turned[0:rows, g0:g0 + ng, :],
                    ).then_inc(x0_stored, 16)

            sp.dma_start(ids_sb[:, :], ids[0:BT, :]).then_inc(first_ids_loaded, 16)
            sp.dma_start(hot_ids, bass.AP(ids_hot.tensor, 0, [[0, VP], [1, len(HOT) * BT]])).then_inc(hot_ids_loaded, 16)
            sp.dma_start(hot_rows, table_rows).then_inc(hot_ids_loaded, 16)
            for n, f in enumerate(HOT):
                assert tables[f].shape[0] == VP * VB
                sp.dma_start(hot_tables[:, n, :, :], tables[f].rearrange("(p k) d -> p k d", k=VB)).then_inc(hot_tables_loaded, 16)
            sp.dma_start(w1s_sb, w1s).then_inc(w1s_loaded, 16)
            for dst, src in ((w0a_sb, w0a), (w0b_sb, w0b), (bias[:, 0:1], b0), (bias[:, 1:2], b1),
                             (bias[:, 2:3], b2), (bias[:, 4:4 + C1], bt1), (bias[:, 4 + C1:4 + C1 + C2], bt2),
                             (w1_sb[:, :, :], w1), (w2_sb[:, :, :], w2), (wt1_sb[:, :, :], wt1),
                             (wt1d_sb, wt1d), (wt2_sb[:, :, :], wt2), (wt3_sb[:, :], wt3)):
                sp.dma_start(dst, src).then_inc(weights_loaded, 16)

            store_x0(0)
            sp.wait_ge(x0_stored, 64)
            load_l0_first()
            sp.wait_ge(w_lo_made, 2)
            load_l0(0, 1, l0_left_early, l0_right_early)
            load_wide(0, 0, 0)
            sp.wait_ge(x1_kept, 1)
            store_x1(0, 0)
            load_left(0, 0, 0)
            sp.wait_ge(x1_stored[0], 16)
            sp.wait_ge(products_made, LEAD + L0_ITEMS)
            load_right(0, 0, 0)
            load_left(0, 0, 1)
            load_right(0, 0, 1)

            def tile(t, first=False, last=False):
                for q in range(Q):
                    i = q * CI
                    nt, nq = (t, q + 1) if q + 1 < Q else (t + 1, 0)
                    nnt, nnq = (t, q + 2) if q + 2 < Q else (t + 1, q + 2 - Q)
                    if not (last and q + 2 >= Q):
                        sp.wait_ge(products_made, items_made(t, i + L0_ITEMS - 1))
                        load_l0(nnt, nnq)
                    if not (last and q == Q - 1):
                        sp.wait_ge(x1_kept, Q * t + q + 2)
                        store_x1(nt, nq)
                    if q == Q - 1:
                        if last:
                            sp.wait_ge(pair_turned, NP * t)
                        sp.dma_start(x0_cols.unsqueeze(1), x0_rows[bass.ds(t, 1), 0:F, :].rearrange("o f n -> f o n")
                                     ).then_inc(x0_cols_loaded, 16)
                    sp.wait_ge(products_made, items_made(t, i + WIDE[0], last))
                    load_wide(t, q, 1)
                    if q == 0 and not last:
                        store_x0(t + 1)
                    if not (last and q == Q - 1):
                        sp.wait_ge(hi_made, items_made(t, i + WIDE[1] - 1))
                        load_right(nt, nq, 0)
                        sp.wait_ge(products_made, items_made(t, i + WIDE[1]))
                        load_wide(nt, nq, 0)
                        sp.wait_ge(products_made, items_made(t, i + WIDE[1] + LG[0]))
                        load_left(nt, nq, 0)
                        sp.wait_ge(products_made, items_made(t, i + CI - 1))
                        load_left(nt, nq, 1)
                        load_right(nt, nq, 1)
                    if q == Q - 1:
                        if not first:
                            sp.wait_ge(y_kept, t)
                            sp.dma_start(y_out[:, bass.ds((t - 1) * BT, BT)], y_sb[:, :]).then_inc(y_stored, 16)
                        sp.dma_start(dense_sb, dense_t[:, bass.ds(t * BT, BT)]).then_inc(dense_loaded, 16)

            tile(0, first=True)
            with sp.Fori(1, T - 1) as t:
                tile(t)
            tile(T - 1, last=True)
            sp.wait_ge(y_kept, T)
            sp.dma_start(y_out[:, (T - 1) * BT:], y_sb[:, :]).then_inc(y_stored, 16)
            sp.wait_ge(y_stored, 16 * T)

        @block.gpsimd
        def _(pool):
            nc.gpsimd.memset(eye[:, :], 0.0).then_inc(eye_made, 1)
            pool.wait_ge(eye_made, 1)
            nc.gpsimd.affine_select(out=eye[:, :], in_=eye[:, :], compare_op=ALU.not_equal, fill=1.0, base=0,
                                    pattern=[[-1, 128]], channel_multiplier=1).then_inc(eye_made, 1)

            def gather(fields):
                for f in fields:
                    pool.indirect_dma_start(
                        out=emb[:, f, :], out_offset=None, in_=tables[f],
                        in_offset=bass.IndirectOffsetOnAxis(ap=ids_sb[:, f:f + 1], axis=0),
                    ).then_inc(emb_gathered, 16)

            pool.wait_ge(first_ids_loaded, 16)
            gather([f for f in range(F) if f not in HOT])
            with pool.Fori(16, 16 * (T - 1) + 1, 16) as t16:
                pool.wait_ge(emb_turned, t16 // 16)
                pool.dma_start(ids_sb[:, :], ids[bass.ds(t16 * (BT // 16), BT), :]).then_inc(ids_loaded, 16)
                pool.wait_ge(eye_made, 2)
                pool.wait_ge(ids_loaded, t16)
                gather(range(F))

        @block.scalar
        def _(act):
            def keep_x0(t):
                act.wait_ge(emb_turned, t + 1)
                if not isinstance(t, int) or t > 0:
                    act.wait_ge(x0_stored, 64 * t)
                nc.scalar.activation(x0_turned[:, 0:NX - 1, :], g_ps[:, 0, :].rearrange("p (g b) -> p g b", b=BT), ACT.Copy)
                nc.scalar.activation(x0_turned[0:XLAST, NX - 1, :], g_ps[0:XLAST, 1, 0:BT], ACT.Copy).then_inc(x0_kept, 1)

            def keep_x1(t, q, used, early=False):
                act.wait_ge(products_used, used)
                if not early:
                    act.wait_ge(x1_stored[q % 2], 16 * (2 * t + q // 2))
                    act.wait_ge(x1_summed, Q * t + q - 1)
                nc.scalar.activation(x1[:, q % 2, :], x1_ps[:, :], ACT.Identity, bias=bias[:, 0:1]).then_inc(x1_kept, 1)

            def keep_x2(t, q, last=False):
                act.wait_ge(products_used, items_made(t, q * CI + CI - 1, last))
                nc.scalar.activation(x2[:, q * N:(q + 1) * N], x2_ps[:, q % 2, :], ACT.Identity,
                                     bias=bias[:, 1:2]).then_inc(x2_kept, 1)

            def place_diag(p, b):
                return nc.scalar.activation(x0_diag[:, :, 0:F, b],
                                            turn_ps[:, 2 * H:2 * H + 2 * F].rearrange("p (i j) -> p i j", i=2),
                                            ACT.Copy, scale=x0_diag[:, 0, F, b:b + 1])

            def tail(n, i):
                if i in TURN:
                    p = TURN.index(i)
                    act.wait_ge(pair_turned, NP * n + p + 1)
                    nc.scalar.activation(x2_turned[:, :, :], turn_ps[:, 0:2 * H].rearrange("p (i h) -> p i h", i=2),
                                         ACT.Copy)
                    for b in range(SB // 2):
                        place_diag(p, b)
                if i - 1 in TURN:
                    p = TURN.index(i - 1)
                    for b in range(SB // 2, SB):
                        end = place_diag(p, b)
                    end.then_inc(pair_kept, 1)
                if i in CONTRACT:
                    p = CONTRACT.index(i)
                    act.wait_ge(g_made, NP * n + p + 1)
                    nc.scalar.activation(
                        g_by_sample[:, 2 * p:2 * p + 2, :, :],
                        g_ps[:, :, 0:FS * SB].rearrange("k i (j b) -> k i j b", b=SB), ACT.Copy).then_inc(g_kept, 1)
                if i == L2[-1]:
                    act.wait_ge(z3_made, n + 1)
                    nc.scalar.activation(z3[:, :], z3_ps[:, 0:BT], ACT.Identity, bias=bias[:, 3:4]).then_inc(z3_kept, 1)
                if i == MLP1[-1]:
                    act.wait_ge(h1_made, n + 1)
                    for m in range(C1):
                        end = nc.scalar.activation(h1[:, m, :], mlp_ps[:, m * BT:(m + 1) * BT], ACT.Relu,
                                                   bias=bias[:, 4 + m:5 + m])
                    end.then_inc(h1_kept, 1)
                if i == MLP2[-1]:
                    act.wait_ge(h2_made, n + 1)
                    for m in range(C2):
                        end = nc.scalar.activation(h2[:, m, :], mlp_ps[:, m * BT:(m + 1) * BT], ACT.Relu,
                                                   bias=bias[:, 4 + C1 + m:5 + C1 + m])
                    end.then_inc(h2_kept, 1)
                if i == MLP3:
                    act.wait_ge(y_made, n + 1)
                    nc.scalar.activation(y_sb[:, :], mlp_ps[0:1, 0:BT], ACT.Copy).then_inc(y_kept, 1)
                if i == ITEMS - 1:
                    act.wait_ge(y_stored, 16 * (n + 1))

            def split_item(t, i, last=False):
                n, whole = tiles_of(i)
                rows = P0 if is_l0(i) else 128
                act.wait_ge(products_made, items_made(t, i, last))
                free = slot_free(t, i, 2, last)
                if free is not None:
                    act.wait_ge(products_used, free)
                nc.scalar.activation(products_hi[0:rows, i % 2, :, :], products[0:rows, i % RING, whole:n, :],
                                     ACT.Copy).then_inc(hi_made, 1)

            act.wait_ge(b2_scaled, 1)
            act.wait_ge(mask_made, 2)
            act.wait_ge(w0_folded, 3)
            nc.scalar.activation(w0_hi[:, 0:SPLIT, :], w0a_sb[:, HALF - SPLIT:HALF, :], ACT.Copy)
            nc.scalar.activation(w0_hi[:, SPLIT:, :], w0a_sb[:, NT0 - SPLIT:, :], ACT.Copy).then_inc(w_hi_made, 1)
            act.wait_ge(w1s_loaded, 16)
            nc.scalar.activation(w1_hi[:, :, :], w1s_sb, ACT.Copy).then_inc(w_hi_made, 1)
            act.wait_ge(one_hot_used, len(HOT))
            n = 0
            for f0, f1 in HOT_RUNS:
                end = nc.scalar.activation(emb[:, f0:f1, :], hot_ps[:, n:n + f1 - f0, :], ACT.Copy)
                n += f1 - f0
            end.then_inc(hot_kept, 1)
            keep_x0(0)
            for i in FIRST:
                split_item(0, i)
            keep_x1(0, 0, LEAD, early=True)
            for i in (0, 1):
                split_item(0, i)

            def tile(t, first=False, last=False):
                for i in range(ITEMS):
                    q = i // CI
                    if i % CI == WIDE[1] - 3 and not (last and q == Q - 1):
                        nt, nq = (t, q + 1) if q + 1 < Q else (t + 1, 0)
                        act.wait_ge(x1_stored[nq % 2], 16 * (2 * nt + nq // 2 + 1))
                    if i + 2 >= ITEMS:
                        if not last:
                            split_item(t + 1, i + 2 - ITEMS)
                    elif not skipped(i + 2, last):
                        split_item(t, i + 2, last)
                    if i % CI == L0_ITEMS - 1 and not skipped(i, last):
                        if q + 1 < Q:
                            if q == 1 and not last:
                                act.wait_ge(x0_stored, 64 * (t + 2))
                            keep_x1(t, q + 1, items_made(t, i, last), early=first and q == 0)
                        else:
                            keep_x1(t + 1, 0, items_made(t, i, last))
                    if i == (FIRST_TURN_EMB if first else TURN_EMB) and not last:
                        keep_x0(t + 1)
                    if not first:
                        tail(t - 1, i)
                    if i == KEEP_X2:
                        keep_x2(t, 0, last)
                    if i % CI == CI - 1 and q > 0:
                        keep_x2(t, q, last)

            tile(0, first=True)
            with act.Fori(1, T - 1) as t:
                tile(t)
            tile(T - 1, last=True)
            def keep_last_g(p):
                act.wait_ge(last_g_made[0], p + 1)
                nc.scalar.activation(g_by_sample[:, 2 * p, :, :], g_ps[:, 0, 0:FS * SB].rearrange("k (j b) -> k j b", b=SB),
                                     ACT.Copy).then_inc(last_g_kept[0], 1)

            for p in range(NP):
                act.wait_ge(last_x2_turned, p + 1)
                if p >= 2:
                    act.wait_ge(last_g_made[1], p - 1)
                nc.scalar.activation(last_x2s[p % 2], x2_banks[p % 2][:, 0:2 * H].rearrange("p (i h) -> p i h", i=2),
                                     ACT.Copy).then_inc(last_x2_kept, 1)
                if p > 0:
                    keep_last_g(p - 1)
            keep_last_g(NP - 1)
            for i in range(Z1_IN, MLP3 + 1):
                tail(T - 1, i)

        @block.vector
        def _(dve):
            dve.wait_ge(hot_ids_loaded, 32)
            for n in range(len(HOT)):
                if n >= HOT_RING:
                    dve.wait_ge(one_hot_used, n - HOT_RING + 1)
                nc.vector.tensor_tensor(one_hot[:, n % HOT_RING, :, :],
                                        hot_ids[:, n * BT:(n + 1) * BT].unsqueeze(1).broadcast_to([VP, VB, BT]),
                                        hot_rows.unsqueeze(2).broadcast_to([VP, VB, BT]), ALU.is_equal).then_inc(one_hot_made, 1)
            dve.wait_ge(weights_loaded, 16 * 13)
            dve.wait_ge(w1s_loaded, 16)
            whole = HALF - SPLIT
            nc.vector.tensor_tensor(w0_sb[:, 0:whole, :], w0a_sb[:, 0:whole, :], w0b_sb[:, 0:whole, :], ALU.add).then_inc(w0_folded, 1)
            nc.vector.tensor_tensor(w0_sb[:, whole:, :], w0a_sb[:, HALF:NT0 - SPLIT, :], w0b_sb[:, HALF:NT0 - SPLIT, :],
                                    ALU.add).then_inc(w0_folded, 1)
            dve.wait_ge(w0_folded, 2)
            nc.vector.tensor_tensor(w0a_sb, w0a_sb, w0b_sb, ALU.add).then_inc(w0_folded, 1)
            nc.vector.tensor_scalar(bias[:, 3:4], bias[:, 2:3], float(D), None, ALU.mult).then_inc(b2_scaled, 1)
            dve.wait_ge(eye_made, 2)
            nc.vector.tensor_reduce(x0_diag[:, 0, F, :], eye[:, :].rearrange("p (d b) -> p b d", b=SB),
                                    AX.X, ALU.add).then_inc(mask_made, 1)
            dve.wait_ge(mask_made, 1)
            nc.vector.tensor_copy(x0_diag[:, 1, F, :], x0_diag[:, 0, F, :]).then_inc(mask_made, 1)

            dve.wait_ge(w_hi_made, 1)
            nc.vector.tensor_tensor(w0_lo[:, 0:SPLIT, :], w0a_sb[:, HALF - SPLIT:HALF, :], w0_hi[:, 0:SPLIT, :].bitcast(fp32), ALU.subtract)
            nc.vector.tensor_tensor(w0_lo[:, SPLIT:, :], w0a_sb[:, NT0 - SPLIT:, :], w0_hi[:, SPLIT:, :].bitcast(fp32),
                                    ALU.subtract).then_inc(w_lo_made, 1)
            dve.wait_ge(w_hi_made, 2)
            nc.vector.tensor_tensor(w1_lo[:, :, :], w1s_sb, w1_hi[:, :, :].bitcast(fp32), ALU.subtract).then_inc(w_lo_made, 1)

            def multiply(t, i):
                q, n = i // CI, tiles_of(i)[0]
                slot = i % RING
                if is_l0(i):
                    at = HALF * (i % CI)
                    if i in FIRST:
                        dve.wait_ge(l0_first_loaded[FIRST.index(i)], 16 * (1 + ND if i == FIRST[0] else ND))
                    elif i % CI == 0:
                        dve.wait_ge(l0_loaded, 16 * (1 + ND) * (Q * t + q + 1))
                    early = isinstance(t, int) and t == 0 and i in (0, 1)
                    left, right = (l0_left_early, l0_right_early) if early else (l0_left[:, :], l0_right[:, :, :])
                    right = right[:, at:at + n, :]
                    out = products[0:P0, slot, 0:n, :]
                else:
                    half, g = l1_item(i)
                    c = Q * t + q + 1
                    if g < 0:
                        dve.wait_ge(wide_loaded[half], 16 * c)
                        left, right = x1[:, q % 2, :], wide_left[:, 0:n, :]
                    else:
                        if half == 0 and g == 0:
                            dve.wait_ge(left_loaded[0], 16 * LG[0] * c)
                        if half == 0 and g == LG[0]:
                            dve.wait_ge(left_loaded[1], 16 * LG[1] * c)
                        if g == 0:
                            dve.wait_ge(right_loaded[half], 16 * c)
                        left, right = l1_left[:, g, :], l1_right[:, HALF * half:HALF * (half + 1), :]
                    out = products[:, slot, 0:n, :]
                nc.vector.tensor_tensor(out, left.unsqueeze(1).broadcast_to([left.shape[0], n, N]), right,
                                        ALU.mult).then_inc(products_made, 1)

            def split_item(t, i, last=False):
                n, whole = tiles_of(i)
                rows = P0 if is_l0(i) else 128
                dve.wait_ge(hi_made, items_made(t, i, last))
                nc.vector.tensor_tensor(products_lo[0:rows, i % 2, :, :], products[0:rows, i % RING, whole:n, :],
                                        products_hi[0:rows, i % 2, :, :].bitcast(fp32), ALU.subtract).then_inc(lo_made, 1)

            def sum_x1(t, q):
                dve.wait_ge(x1_kept, Q * t + q + 1)
                if q == 0 and not (isinstance(t, int) and t == 0):
                    dve.wait_ge(z1_made, t)
                nc.vector.tensor_reduce(z1_parts[:, q, :], x1[:, q % 2, :].rearrange("h (d b) -> h b d", b=BT),
                                        AX.X, ALU.add).then_inc(x1_summed, 1)

            def sum_z1(t):
                dve.wait_ge(x1_summed, Q * t + Q)
                if not isinstance(t, int) or t > 0:
                    dve.wait_ge(z1_read, t)
                nc.vector.tensor_reduce(z1[:, :], z1_parts[:, :, :].rearrange("h q b -> h b q"),
                                        AX.X, ALU.add).then_inc(z1_made, 1)

            for i in FIRST:
                multiply(0, i)
            for i in FIRST:
                split_item(0, i)

            def tile(t, first=False, last=False):
                for i in range(ITEMS):
                    q, r = i // CI, i % CI
                    if not skipped(i, last):
                        free = slot_free(t, i, RING, last)
                        if free is not None:
                            dve.wait_ge(products_used, free)
                        multiply(t, i)
                        if not skipped(i - 1, last) and not (first and i == 0):
                            split_item(t, i - 1, last)
                    elif i % CI == 0:
                        split_item(t, i - 1)
                    if first and i == 1:
                        sum_x1(0, 0)
                    if q + 1 < Q and r == L0_ITEMS + RING:
                        sum_x1(t, q + 1)
                    if i == SUM_Z1:
                        sum_z1(t)
                    if i == SUM_Z1 + 1 and not last:
                        sum_x1(t + 1, 0)

            tile(0, first=True)
            with dve.Fori(1, T - 1) as t:
                tile(t)
            tile(T - 1, last=True)
            split_item(T - 1, ITEMS - 1, last=True)

            def keep_last_g(p):
                dve.wait_ge(last_g_made[1], p + 1)
                nc.vector.tensor_copy(g_by_sample[:, 2 * p + 1, :, :], g_ps[:, 1, 0:FS * SB].rearrange("k (j b) -> k j b", b=SB)
                                      ).then_inc(last_g_kept[1], 1)

            dve.wait_ge(last_x0_turned, 1)
            for k in range(2):
                nc.vector.tensor_copy(last_diags[1][:, k, F, :], x0_diag[:, k, F, :]).then_inc(last_mask_made, 1)
            dve.wait_ge(last_mask_made, 2)
            for p in range(NP):
                dve.wait_ge(last_x0_turned, p + 1)
                if p >= 2:
                    dve.wait_ge(last_g_made[1], p - 1)
                for k in range(2):
                    end = nc.vector.tensor_tensor(
                        last_diags[p % 2][:, k, 0:F, :],
                        x0_banks[p % 2][:, k * F:(k + 1) * F].unsqueeze(2).broadcast_to([128, F, SB]),
                        last_diags[p % 2][:, k, F, :].unsqueeze(1).broadcast_to([128, F, SB]), ALU.mult)
                end.then_inc(last_diag_made, 1)
                if p > 0:
                    keep_last_g(p - 1)
            keep_last_g(NP - 1)

        @block.tensor
        def _(pe):
            mm = nc.tensor.matmul

            def turn_emb(t):
                pe.wait_ge(emb_gathered, 16 * (F * (t + 1) - len(HOT)))
                flat = emb[:, :, :].rearrange("b f d -> b (f d)")
                for g in range(NX):
                    rows = XLAST if g == NX - 1 else 128
                    last = nc.tensor.transpose(g_ps[0:rows, g // 4, (g % 4) * BT:(g % 4 + 1) * BT],
                                               flat[:, 128 * g:128 * g + rows], eye[:, :])
                last.then_inc(emb_turned, 1)

            def contract(out, w, w_hi, w_lo, at, at_split, rows, i, made, first, last):
                n, whole = tiles_of(i)
                for k in range(whole):
                    mm(out, w[:, at + k, :], products[0:rows, i % RING, k, :], start=first and k == 0, stop=False)
                pe.wait_ge(lo_made, made)
                for k in range(SPLIT):
                    hi = products_hi[0:rows, i % 2, k, :]
                    mm(out, w_hi[:, at_split + k, :], hi, start=False, stop=False)
                    mm(out, w_hi[:, at_split + k, :], products_lo[0:rows, i % 2, k, :], start=False, stop=False)
                    end = mm(out, w_lo[:, at_split + k, :], hi, start=False, stop=last and k == SPLIT - 1)
                end.then_inc(products_used, 1)

            def layer0(t, i, made):
                c = Q * t + i // CI + 1
                half = i % CI
                pe.wait_ge(products_made, made)
                if half == 0 and not (isinstance(c, int) and c < 1):
                    pe.wait_ge(x1_kept, c)
                contract(x1_ps[:, :], w0_sb, w0_hi, w0_lo, (HALF - SPLIT) * half, SPLIT * half, P0, i, made,
                         half == 0, half == 1)

            def layer1(t, i, made):
                q = i // CI
                c = Q * t + q
                pe.wait_ge(products_made, made)
                if i % CI == L0_ITEMS and not (isinstance(c, int) and c < 2):
                    pe.wait_ge(x2_kept, c - 1)
                at = i % CI - L0_ITEMS
                whole = sum(tiles_of(n)[1] for n in range(L0_ITEMS, i % CI))
                contract(x2_ps[:, q % 2, :], w1_sb, w1_hi, w1_lo, whole, SPLIT * at, 128, i, made,
                         i % CI == L0_ITEMS, i % CI == CI - 1)

            def tail(n, i, last=False):
                if i in TURN:
                    p = TURN.index(i)
                    if p == 0:
                        pe.wait_ge(x2_kept, Q * (n + 1))
                        pe.wait_ge(x0_cols_loaded, 16 * (n + 1))
                    for k in range(2):
                        nc.tensor.transpose(turn_ps[:, k * H:(k + 1) * H], x2[:, 2 * p + k::GROUPS], eye[:, :])
                    for k in range(2):
                        end = nc.tensor.transpose(turn_ps[:, 2 * H + k * F:2 * H + (k + 1) * F],
                                                  x0_cols[:, 2 * p + k::GROUPS], eye[0:F, 0:F])
                    end.then_inc(pair_turned, 1)
                if i in CONTRACT:
                    p = CONTRACT.index(i)
                    pe.wait_ge(pair_kept, NP * n + p + 1)
                    if p > 0:
                        pe.wait_ge(g_kept, NP * n + p)
                    for k in range(2):
                        end = mm(g_ps[:, k, 0:FS * SB], x2_turned[:, k, :],
                                 x0_diag[:, k, :, :].rearrange("p j b -> p (j b)"), start=True, stop=True)
                    end.then_inc(g_made, 1)
                if i == Z1_IN:
                    pe.wait_ge(z1_made, n + 1)
                    for m in range(C1):
                        end = mm(mlp_ps[:, m * BT:(m + 1) * BT], wt1_sb[:, 0, 128 * m:128 * (m + 1)], z1[:, :],
                                 start=m == 0, stop=False)
                    end.then_inc(z1_read, 1)
                if i in L2:
                    part = L2.index(i)
                    if part == 0 and not last:
                        pe.wait_ge(g_kept, NP * (n + 1))
                    for j in range(F * part // len(L2), F * (part + 1) // len(L2)):
                        end = mm(z3_ps[:, 0:BT], w2_sb[:, j, :], g_sb[:, j, :], start=j == 0, stop=j == F - 1)
                    if part == len(L2) - 1:
                        end.then_inc(z3_made, 1)
                if i in MLP1:
                    m = MLP1.index(i)
                    if m == 0:
                        pe.wait_ge(z3_kept, n + 1)
                        pe.wait_ge(dense_loaded, 16 * (n + 1))
                    out = mlp_ps[:, m * BT:(m + 1) * BT]
                    cols = slice(128 * m, 128 * (m + 1))
                    mm(out, wt1_sb[:, 1, cols], g_sb[:, F, :], start=False, stop=False)
                    mm(out, wt1d_sb[:, cols], dense_sb, start=False, stop=False)
                    end = mm(out, wt1_sb[:, 2, cols], z3[:, :], start=False, stop=m == C1 - 1)
                    if m == C1 - 1:
                        end.then_inc(h1_made, 1)
                if i in MLP2:
                    m = MLP2.index(i)
                    if m == 0:
                        pe.wait_ge(h1_kept, n + 1)
                    for k in range(C1):
                        end = mm(mlp_ps[:, m * BT:(m + 1) * BT], wt2_sb[:, k, 128 * m:128 * (m + 1)], h1[:, k, :],
                                 start=k == 0, stop=k == C1 - 1)
                    if m == C2 - 1:
                        end.then_inc(h2_made, 1)
                if i == MLP3:
                    pe.wait_ge(h2_kept, n + 1)
                    for k in range(C2):
                        end = mm(mlp_ps[0:1, 0:BT], wt3_sb[:, k:k + 1], h2[:, k, :], start=k == 0, stop=k == C2 - 1)
                    end.then_inc(y_made, 1)

            for n in range(len(HOT)):
                pe.wait_ge(one_hot_made, n + 1)
                if n == 0:
                    pe.wait_ge(hot_tables_loaded, 16 * len(HOT))
                for k in range(VB):
                    end = mm(hot_ps[:, n, :], one_hot[:, n % HOT_RING, k, :], hot_tables[:, n, k, :],
                             start=k == 0, stop=k == VB - 1)
                end.then_inc(one_hot_used, 1)
            pe.wait_ge(eye_made, 2)
            pe.wait_ge(hot_kept, 1)
            turn_emb(0)
            pe.wait_ge(w_lo_made, 2)
            pe.wait_ge(x0_stored, 64)
            for _ in range(WARM):
                mm(x2_ps[:, 0, :], w2_sb[:, 0, :], w2_sb[:, 0:4, :].rearrange("p j h -> p (j h)"), start=True, stop=True)
            for i in FIRST:
                layer0(0, i, items_made(0, i))

            def tile(t, first=False, last=False):
                for i in range(ITEMS):
                    if not skipped(i, last):
                        (layer0 if is_l0(i) else layer1)(t, i, items_made(t, i, last))
                    if i == (FIRST_TURN_EMB if first else TURN_EMB) and not last:
                        turn_emb(t + 1)
                    if i == CONTRACT[0] and not (first or last):
                        pe.wait_ge(x0_kept, t + 2)
                    if not first:
                        tail(t - 1, i)

            tile(0, first=True)
            with pe.Fori(1, T - 1) as t:
                tile(t)
            tile(T - 1, last=True)

            def contract_last(p):
                pe.wait_ge(last_x2_kept, p + 1)
                pe.wait_ge(last_diag_made, p + 1)
                for k in range(2):
                    if p > 0:
                        pe.wait_ge(last_g_kept[k], p)
                    mm(g_ps[:, k, 0:FS * SB], last_x2s[p % 2][:, k, :],
                       last_diags[p % 2][:, k, :, :].rearrange("p j b -> p (j b)"), start=True, stop=True).then_inc(last_g_made[k], 1)

            for p in range(NP):
                if p == 0:
                    pe.wait_ge(x0_cols_loaded, 16 * T)
                if p >= 2:
                    pe.wait_ge(last_diag_made, p - 1)
                for k in range(2):
                    end = nc.tensor.transpose(x0_banks[p % 2][:, k * F:(k + 1) * F], x0_cols[:, 2 * p + k::GROUPS], eye[0:F, 0:F])
                end.then_inc(last_x0_turned, 1)
                if p == 0:
                    pe.wait_ge(x2_kept, Q * T)
                if p >= 2:
                    pe.wait_ge(last_x2_kept, p - 1)
                for k in range(2):
                    end = nc.tensor.transpose(x2_banks[p % 2][:, k * H:(k + 1) * H], x2[:, 2 * p + k::GROUPS], eye[:, :])
                end.then_inc(last_x2_turned, 1)
                if p > 0:
                    contract_last(p - 1)
            contract_last(NP - 1)
            for k in range(2):
                pe.wait_ge(last_g_kept[k], NP)
            for i in range(Z1_IN, MLP3 + 1):
                tail(T - 1, i, last=True)


def kernel(**inputs):
    import numpy as np
    import concourse.bacc as bacc
    from concourse.bass_utils import run_bass_kernel_spmd

    W0 = np.asarray(inputs["L0_rec_W0"]).reshape(H, F, F)
    W1 = np.asarray(inputs["L0_rec_W1"]).reshape(H, F, H)
    W2 = np.asarray(inputs["L0_rec_W2"]).reshape(H, F, H)
    Wt1 = np.asarray(inputs["W_top1"])
    Wt2 = np.asarray(inputs["W_top2"])

    j = np.arange(F)[None, :, None]
    delta = np.arange(NT0)[None, None, :] * ND + np.arange(ND)[:, None, None]
    k = (j + delta) % F
    j = np.broadcast_to(j, k.shape)
    w0a = np.zeros((ND, F, NT0, H), W0.dtype)
    w0b = np.zeros((ND, F, NT0, H), W0.dtype)
    once = np.broadcast_to(delta <= F // 2, k.shape)
    both = once & np.broadcast_to(delta > 0, k.shape)
    w0a[once] = W0[:, j[once], k[once]].T
    w0b[both] = W0[:, k[both], j[both]].T

    w1, w1s = [], []
    for i in range(L0_ITEMS, CI):
        half, g = l1_item(i)
        n, whole = tiles_of(i)
        if g < 0:
            j = NG * JJ + half * HALF
            tiles = W1[:, j:j + n, :].transpose(2, 1, 0)
        else:
            tiles = W1[:, JJ * g:JJ * (g + 1), HALF * KK * half:HALF * KK * (half + 1)]
            tiles = tiles.reshape(H, JJ, KK, HALF).transpose(1, 2, 3, 0).reshape(128, HALF, H)
        w1.append(tiles[:, :whole])
        w1s.append(tiles[:, whole:])

    arrays = {
        "ids": np.asarray(inputs["ids"]),
        "ids_hot": np.asarray(inputs["ids"])[:BT, list(HOT)].T,
        "table_rows": np.arange(VP * VB, dtype=np.int32).reshape(VP, VB),
        "dense_t": np.asarray(inputs["dense_ctx"]).T,
        "w0a": w0a.reshape(P0, NT0, H),
        "w0b": w0b.reshape(P0, NT0, H),
        "b0": np.asarray(inputs["L0_rec_b0"]).reshape(H, 1),
        "w1": np.concatenate(w1, axis=1),
        "w1s": np.concatenate(w1s, axis=1),
        "b1": np.asarray(inputs["L0_rec_b1"]).reshape(H, 1),
        "w2": W2.transpose(2, 1, 0),
        "b2": np.asarray(inputs["L0_rec_b2"]).reshape(H, 1),
        "wt1": Wt1[:3 * H].reshape(3, H, M1).transpose(1, 0, 2),
        "wt1d": Wt1[3 * H:],
        "bt1": np.asarray(inputs["b_top1"]).reshape(C1, 128).T,
        "wt2": Wt2.reshape(C1, 128, M2).transpose(1, 0, 2),
        "bt2": np.asarray(inputs["b_top2"]).reshape(C2, 128).T,
        "wt3": np.asarray(inputs["W_top3"]).reshape(C2, 128).T,
    }
    for f in range(F):
        arrays[f"tbl_{f}"] = np.asarray(inputs[f"tbl_{f}"])

    nc = bacc.Bacc("TRN2", target_bir_lowering=False, num_devices=1)
    aps = {}
    for name in arrays:
        arrays[name] = np.ascontiguousarray(arrays[name])
        aps[name] = nc.dram_tensor(f"in_{name}", arrays[name].shape, mybir.dt.from_np(arrays[name].dtype),
                                   kind="ExternalInput").ap()
    y_out = nc.dram_tensor("out_y", (1, B), mybir.dt.float32, kind="ExternalOutput").ap()
    build(nc, aps["ids"], aps["ids_hot"], aps["table_rows"], [aps[f"tbl_{f}"] for f in range(F)], *[aps[n] for n in (
        "dense_t", "w0a", "w0b", "b0", "w1", "w1s", "b1", "w2", "b2", "wt1", "wt1d", "bt1", "wt2", "bt2", "wt3")], y_out)
    r = run_bass_kernel_spmd(nc, [{f"in_{name}": a for name, a in arrays.items()}], core_ids=[0])
    return r.results[0]["out_y"].reshape(B, 1)
```
